# Optimizing a Trainium2 kernel written in Bass

```python
import numpy as np
import jax
import jax.numpy as jnp

def _softmax(x, axis=-1):
    return jax.nn.softmax(x, axis=axis)

def _gelu(x):
    return jax.nn.gelu(x, approximate=True)

def _silu(x):
    return jax.nn.silu(x)

def _sigmoid(x):
    return jax.nn.sigmoid(x)

def _layernorm(x, axis=-1, eps=1e-05):
    m = jnp.mean(x, axis=axis, keepdims=True)
    v = jnp.var(x, axis=axis, keepdims=True)
    return (x - m) / jnp.sqrt(v + eps)

def _scatter_add(tgt, idx, src, axis=0):
    return tgt.at[idx].add(src)

def _segment_sum(src, seg, n):
    return jax.ops.segment_sum(src, seg, n)
kernel_name = 'mk_adj_resnorm_d4_adj_r2_4762b4'

def setup_inputs(seed: int=0):
    np.random.seed(seed)
    _w = jnp.asarray

    def _rec_inputs():
        import jax
        import jax.numpy as jnp
        _gk = jax.random.key(seed)
        x = -0.0005207 + 1.001 * jax.random.normal(jax.random.fold_in(_gk, 1), (16, 512, 128), jnp.float32)
        _w = (1.0 + jnp.arange(512, dtype=jnp.float32)) ** (-0.5)
        _w = _w / _w.mean()
        _pij = jnp.clip(0.03125 * _w[:, None] * _w[None, :], 0.0, 1.0)
        _a = jax.random.uniform(jax.random.fold_in(_gk, 2), (16, 512, 512)) < _pij
        _a = jnp.logical_or(_a, jnp.swapaxes(_a, -1, -2))
        _a = jnp.logical_or(_a, jnp.eye(512, dtype=bool))
        _af = _a.astype(jnp.float32)
        _af = _af * jax.random.uniform(jax.random.fold_in(_gk, 3), (16, 512, 512), jnp.float32, 0.05, 1)
        adj = _af
        _nm = jnp.ones((16, 512), dtype=bool)
        nodemask = jnp.where(_nm, 1.0, 0.0).astype(jnp.float32)
        return (x, adj, nodemask)
    x, adj, nodemask = _rec_inputs()

    def _L0_gnn_setup():
        import jax, jax.numpy as jnp
        import numpy as np
        EPS = 1e-06

        def _normalize(A):
            n = A.shape[-1]
            eye = jnp.eye(n, dtype=A.dtype)
            A_hat = A * (1.0 - eye) + eye
            d = 1.0 / (EPS + jnp.sqrt(jnp.sum(A_hat, axis=2)))
            return A_hat * d[:, :, None] * d[:, None, :]
        key = jax.random.key(seed)
        k1, k2, k3 = jax.random.split(key, 3)
        B, N, F, O = (8, 1024, 128, 128)
        x = jax.random.normal(k1, (B, N, F), dtype=jnp.float32)
        adj = jax.random.uniform(k2, (B, N, N), dtype=jnp.float32)
        kernel = jax.random.normal(k3, (F, O), dtype=jnp.float32) * 0.05
        return {'x': x, 'adj': adj, 'kernel': kernel}
    _L0_gnn_all = _L0_gnn_setup()
    _L0_gnn_in = {k: v for k, v in _L0_gnn_all.items() if k in ('kernel',)}
    del _L0_gnn_all

    def _L1_gnn_setup():
        import jax, jax.numpy as jnp
        import numpy as np
        B, N, C, L = (32, 512, 128, 4)

        def _gru_cell(m, h, w_ih, w_hh, b_ih, b_hh):
            gx = m @ w_ih.T + b_ih
            gh = h @ w_hh.T + b_hh
            xr, xz, xn = jnp.split(gx, 3, axis=-1)
            hr, hz, hn = jnp.split(gh, 3, axis=-1)
            r = jax.nn.sigmoid(xr + hr)
            z = jax.nn.sigmoid(xz + hz)
            n = jnp.tanh(xn + r * hn)
            return (1.0 - z) * n + z * h
        key = jax.random.key(seed)
        ks = jax.random.split(key, 8)
        x = jax.random.normal(ks[0], (B, N, C), dtype=jnp.float32)
        adj = jax.random.randint(ks[1], (B, N, N), 0, 2).astype(jnp.float32)
        mask = jnp.ones((B, N), dtype=jnp.float32)
        s = 1.0 / np.sqrt(C)
        weight = jax.random.uniform(ks[2], (L, C, C), minval=-s, maxval=s, dtype=jnp.float32)
        w_ih = jax.random.uniform(ks[3], (L, 3 * C, C), minval=-s, maxval=s, dtype=jnp.float32)
        w_hh = jax.random.uniform(ks[4], (L, 3 * C, C), minval=-s, maxval=s, dtype=jnp.float32)
        b_ih = jax.random.uniform(ks[5], (L, 3 * C), minval=-s, maxval=s, dtype=jnp.float32)
        b_hh = jax.random.uniform(ks[6], (L, 3 * C), minval=-s, maxval=s, dtype=jnp.float32)
        return {'x': x, 'adj': adj, 'mask': mask, 'weight': weight, 'w_ih': w_ih, 'w_hh': w_hh, 'b_ih': b_ih, 'b_hh': b_hh}
    _L1_gnn_all = _L1_gnn_setup()
    _L1_gnn_in = {k: v for k, v in _L1_gnn_all.items() if k in ('weight', 'w_ih', 'w_hh', 'b_ih', 'b_hh')}
    del _L1_gnn_all

    def _L2_gnn_setup():
        import jax, jax.numpy as jnp
        import numpy as np
        B, N, F, U = (8, 1024, 128, 128)
        EDGE_PROB = 0.01
        key = jax.random.key(seed)
        k1, k2, k3, k4, k5 = jax.random.split(key, 5)
        x = jax.random.normal(k1, (B, N, F), dtype=jnp.float32)
        adj = (jax.random.uniform(k2, (B, N, N)) < EDGE_PROB).astype(jnp.float32)
        W_pre = jax.random.normal(k3, (F, U), dtype=jnp.float32) * 0.1
        a_snd = jax.random.normal(k4, (U,), dtype=jnp.float32) * 0.1
        a_rec = jax.random.normal(k5, (U,), dtype=jnp.float32) * 0.1
        return {'x': x, 'adj': adj, 'W_pre': W_pre, 'a_snd': a_snd, 'a_rec': a_rec}
    _L2_gnn_all = _L2_gnn_setup()
    _L2_gnn_in = {k: v for k, v in _L2_gnn_all.items() if k in ('W_pre', 'a_snd', 'a_rec')}
    del _L2_gnn_all

    def _L3_gnn_setup():
        import jax, jax.numpy as jnp
        import numpy as np
        B, N, F_IN, F_OUT = (4, 2048, 128, 128)
        key = jax.random.key(seed)
        k1, k2, k3 = jax.random.split(key, 3)
        x = jax.random.normal(k1, (B, N, F_IN), dtype=jnp.float32)
        adj = jax.random.uniform(k2, (B, N, N), dtype=jnp.float32)
        weight = jax.random.normal(k3, (F_IN, F_OUT), dtype=jnp.float32) * (6.0 / (F_IN + F_OUT)) ** 0.5
        bias = jnp.zeros((F_OUT,), dtype=jnp.float32)
        return {'x': x, 'adj': adj, 'weight': weight, 'bias': bias}
    _L3_gnn_all = _L3_gnn_setup()
    _L3_gnn_in = {k: v for k, v in _L3_gnn_all.items() if k in ('weight', 'bias')}
    del _L3_gnn_all
    return {'x': x, 'adj': adj, 'nodemask': nodemask, 'L0_gnn_kernel': _L0_gnn_in['kernel'], 'L1_gnn_weight': _L1_gnn_in['weight'], 'L1_gnn_w_ih': _L1_gnn_in['w_ih'], 'L1_gnn_w_hh': _L1_gnn_in['w_hh'], 'L1_gnn_b_ih': _L1_gnn_in['b_ih'], 'L1_gnn_b_hh': _L1_gnn_in['b_hh'], 'L2_gnn_W_pre': _L2_gnn_in['W_pre'], 'L2_gnn_a_snd': _L2_gnn_in['a_snd'], 'L2_gnn_a_rec': _L2_gnn_in['a_rec'], 'L3_gnn_weight': _L3_gnn_in['weight'], 'L3_gnn_bias': _L3_gnn_in['bias']}

def reference(x, adj, nodemask, L0_gnn_kernel, L1_gnn_weight, L1_gnn_w_ih, L1_gnn_w_hh, L1_gnn_b_ih, L1_gnn_b_hh, L2_gnn_W_pre, L2_gnn_a_snd, L2_gnn_a_rec, L3_gnn_weight, L3_gnn_bias):
    import jax
    import jax.numpy as jnp

    def _L0_gnn_ref(x, adj, kernel):
        import jax, jax.numpy as jnp
        import numpy as np
        EPS = 1e-06

        def _normalize(A):
            n = A.shape[-1]
            eye = jnp.eye(n, dtype=A.dtype)
            A_hat = A * (1.0 - eye) + eye
            d = 1.0 / (EPS + jnp.sqrt(jnp.sum(A_hat, axis=2)))
            return A_hat * d[:, :, None] * d[:, None, :]
        norm = _normalize(adj)
        agg = jnp.einsum('bnm,bmf->bnf', norm, x)
        out = jnp.einsum('bnf,fo->bno', agg, kernel)
        return jax.nn.relu(out)

    def _L1_gnn_ref(x, adj, mask, weight, w_ih, w_hh, b_ih, b_hh):
        import jax, jax.numpy as jnp
        import numpy as np
        B, N, C, L = (32, 512, 128, 4)

        def _gru_cell(m, h, w_ih, w_hh, b_ih, b_hh):
            gx = m @ w_ih.T + b_ih
            gh = h @ w_hh.T + b_hh
            xr, xz, xn = jnp.split(gx, 3, axis=-1)
            hr, hz, hn = jnp.split(gh, 3, axis=-1)
            r = jax.nn.sigmoid(xr + hr)
            z = jax.nn.sigmoid(xz + hz)
            n = jnp.tanh(xn + r * hn)
            return (1.0 - z) * n + z * h
        h = x
        for i in range(L):
            hw = jnp.einsum('bnc,cd->bnd', h, weight[i])
            m = jnp.einsum('bjn,bjd->bnd', adj, hw)
            h = _gru_cell(m, h, w_ih[i], w_hh[i], b_ih[i], b_hh[i])
        return h * mask[:, :, None]

    def _L2_gnn_ref(x, adj, W_pre, a_snd, a_rec):
        import jax, jax.numpy as jnp
        import numpy as np
        B, N, F, U = (8, 1024, 128, 128)
        EDGE_PROB = 0.01
        n = adj.shape[1]
        adj = jnp.minimum(1.0, adj + jnp.eye(n, dtype=adj.dtype)[None])
        mask = adj > 0
        h = jnp.einsum('bnf,fu->bnu', x, W_pre)
        e_s = jnp.einsum('bnu,u->bn', h, a_snd)
        e_r = jnp.einsum('bnu,u->bn', h, a_rec)
        logits = e_s[:, :, None] + e_r[:, None, :]
        logits = jax.nn.leaky_relu(logits, negative_slope=0.2)
        neg_inf = jnp.asarray(-1000000000.0, logits.dtype)
        logits = jnp.where(mask, logits, neg_inf)
        att = jax.nn.softmax(logits, axis=1)
        att = jnp.where(mask, att, jnp.asarray(0.0, att.dtype))
        out = jnp.einsum('bsr,bru->bsu', att, h)
        return out

    def _L3_gnn_ref(x, adj, weight, bias):
        import jax, jax.numpy as jnp
        import numpy as np
        B, N, F_IN, F_OUT = (4, 2048, 128, 128)
        degree = jnp.sum(adj, axis=-1)
        d_inv = jnp.power(degree + 1e-06, -0.5)
        adj_norm = d_inv[:, :, None] * adj * d_inv[:, None, :]
        z = jnp.einsum('bnm,bmf->bnf', adj_norm, x)
        z = jnp.einsum('bnf,fo->bno', z, weight) + bias
        return z
    x = _layernorm(x + _L0_gnn_ref(x, adj, L0_gnn_kernel), axis=-1)
    x = _layernorm(x + _L1_gnn_ref(x, adj, nodemask, L1_gnn_weight, L1_gnn_w_ih, L1_gnn_w_hh, L1_gnn_b_ih, L1_gnn_b_hh), axis=-1)
    x = _layernorm(x + _L2_gnn_ref(x, adj, L2_gnn_W_pre, L2_gnn_a_snd, L2_gnn_a_rec), axis=-1)
    x = _layernorm(x + _L3_gnn_ref(x, adj, L3_gnn_weight, L3_gnn_bias), axis=-1)
    return x

_drawn_inputs = setup_inputs


def setup_inputs(seed=0):
    import zlib

    import numpy as np

    out = dict(_drawn_inputs(seed))
    spreads = {'L3_gnn_bias': (0.0, 0.1)}
    factors = {}
    for name, (base, spread) in spreads.items():
        noise = np.random.default_rng([zlib.crc32(name.encode()), seed]).standard_normal(out[name].shape)
        drawn = base * np.exp(spread * noise) if base else spread * noise
        out[name] = jnp.asarray(drawn.astype(out[name].dtype))
    for name, factor in factors.items():
        out[name] = (out[name] * factor).astype(out[name].dtype)
    return out
```

```python
from contextlib import ExitStack

import concourse.bass as bass
from concourse import mybir

ALU = mybir.AluOpType
ACT = mybir.ActivationFunctionType
F32 = mybir.dt.float32
BF16 = mybir.dt.bfloat16
AX_X = mybir.AxisListType.X

P = 128
MASKED = -1e30
LN_EPS = 1e-5
DEG_EPS = 1e-6
SLOPE = 0.2

X, Y = 0, 1

PE_FILL = {
    0: [("post_back", Y)],
    3: [("att_bcast", X)],
    5: [("att_bcast", Y)],
    6: [("att_agg", X)],
    7: [("l0_agg", X), ("att_lin", X)],
    8: [("l0_lin", X)],
    9: [("l3_agg", X)],
    10: [("l3_lin", X), ("att_agg", Y)],
    11: [("att_lin", Y)],
    13: [("l3_agg", Y)],
    14: [("l3_lin", Y), ("l0_agg", Y)],
    15: [("l0_lin", Y)],
}
ACT_FILL = {
    1: [("degree", X)],
    4: [("att_bcast", X)],
    5: [("att_logits", X)],
    6: [("att_bcast", Y)],
    7: [("agg_att", X)],
    8: [("agg_l0", X), ("att_logits", Y)],
    9: [("degree", Y)],
    10: [("agg_l3", X)],
    11: [("agg_att", Y)],
    14: [("agg_l3", Y)],
    15: [("agg_l0", Y)],
}
DVE_FILL = {
    0: [("post_read", X), ("post_res", X), ("post_read", Y)],
    1: [("norm_post", X), ("mask", X)],
    2: [("att_scores", X), ("post_res", Y)],
    3: [("norm_post", Y), ("mask", Y)],
    4: [("att_max", X), ("att_scores", Y)],
    5: [("att_lrelu", X), ("att_weight", X)],
    6: [("l0_degree", X), ("att_max", Y)],
    7: [("l0_scale", X), ("att_lrelu", Y)],
    8: [("att_weight", Y), ("att_res", X)],
    9: [("norm_att", X), ("l0_res", X)],
    10: [("norm_l0", X), ("l0_degree", Y)],
    11: [("l3_res", X), ("att_res", Y), ("l0_scale", Y)],
    12: [("norm_l3", X), ("norm_att", Y)],
    14: [("l3_res", Y)],
    15: [("norm_l3", Y), ("l0_res", Y), ("norm_l0", Y)],
}
POOL_FILL = {
    0: [("rstd_post", X), ("diag_a", X)],
    1: [("diag_at", X), ("mask_diag", X)],
    2: [("rstd_post", Y)],
    3: [("mask_diag", Y)],
    6: [("powers", X)],
    8: [("rstd_att", X), ("diag_a", Y)],
    9: [("rstd_l0", X)],
    10: [("add_bias", X), ("powers", Y)],
    11: [("diag_at", Y), ("rstd_l3", X), ("rstd_att", Y)],
    12: [("add_bias", Y)],
    14: [("rstd_l3", Y)],
    15: [("rstd_l0", Y)],
}


def gnn_kernel(nc, x_in, adj_in, adjt_in, mask_in, k0_in, w1t_in, wiht_in, whht_in, bih_in, bhh_in,
               wpre_in, wpret_in, avec_in, w3_in, bias3_in, out):
    B, _, NT, C = x_in.shape
    N = NT * P
    L = w1t_in.shape[1]
    PAIRS = B // 2
    G = 3 * C
    STEPS = 2 * L
    DVE_LINKS = {"pre": 14, "post": 33}

    with ExitStack() as ctx:
        def sb(name, shape, dtype=F32):
            return ctx.enter_context(nc.sbuf_tensor(name, shape, dtype))

        def bank(name):
            return ctx.enter_context(nc.psum_tensor(name, [P, N], F32))

        def sem(name):
            return ctx.enter_context(nc.semaphore(name))

        ident = sb("ident", [P, P])
        ones = sb("ones", [P, P])
        w1t = sb("w1t", [P, L, C])
        wiht = sb("wiht", [P, L, G])
        whht = sb("whht", [P, L, G])
        wg = sb("wg", [P, L, G])
        bih = sb("bih", [P, L, 3])
        bhh = sb("bhh", [P, L, 3])
        half_b = sb("half_b", [P, L, 3])
        k0 = sb("k0", [P, C])
        wpre = sb("wpre", [P, C])
        wpret = sb("wpret", [P, C])
        w3 = sb("w3", [P, C])
        avec = sb("avec", [P, 2])
        acols = sb("acols", [P, 2, P])
        arow = sb("arow", [P, 2, C])
        bias3 = sb("bias3", [P, C])
        nmask = sb("nmask", [P, B, NT])
        exps = sb("exps", [P, 8])

        a_pre = sb("a_pre", [P, NT, N])
        at_pre = sb("at_pre", [P, NT, N])
        scratch = sb("scratch", [P, NT, N], BF16)
        adiag = sb("adiag", [P, NT, P])
        x0 = [sb(f"x0_{s}", [P, NT, C]) for s in (X, Y)]
        xs_pre = sb("xs_pre", [P, NT, C])
        agg_pre = sb("agg_pre", [P, N])
        y_pre = sb("y_pre", [P, NT, C])
        x1 = [sb(f"x1_{s}", [P, NT, C]) for s in (X, Y)]
        deg = sb("deg", [P, NT])
        ann = sb("ann", [P, NT])
        dd = sb("dd", [P, 8])
        ddp = sb("ddp", [P, 8])
        d0 = sb("d0", [P, NT])
        d3_pre = sb("d3_pre", [P, 2, NT])
        d3_gru = sb("d3_gru", [P, 2, NT])
        d3_post = sb("d3_post", [P, 2, NT])

        a = [sb(f"a_{s}", [P, NT, N]) for s in (X, Y)]
        hT = [sb(f"hT_{s}", [P, N]) for s in (X, Y)]
        hn = [sb(f"hn_{s}", [P, NT, C]) for s in (X, Y)]
        uT = [sb(f"uT_{s}", [P, N]) for s in (X, Y)]
        rg = [sb(f"rg_{s}", [P, N]) for s in (X, Y)]
        zg = [sb(f"zg_{s}", [P, N]) for s in (X, Y)]
        hb = [sb(f"hb_{s}", [P, N]) for s in (X, Y)]
        tg = [sb(f"tg_{s}", [P, N]) for s in (X, Y)]
        ng = [sb(f"ng_{s}", [P, N]) for s in (X, Y)]
        zh = [sb(f"zh_{s}", [P, N]) for s in (X, Y)]

        at = [sb(f"at_{s}", [P, NT, N]) for s in (X, Y)]
        att = [sb(f"att_{s}", [P, NT, N]) for s in (X, Y)]
        es = [sb(f"es_{s}", [P, N]) for s in (X, Y)]
        res = [sb(f"res_{s}", [P, NT, C]) for s in (X, Y)]
        x2 = [sb(f"x2_{s}", [P, NT, C]) for s in (X, Y)]
        x3 = [sb(f"x3_{s}", [P, NT, C]) for s in (X, Y)]
        xs = [sb(f"xs_{s}", [P, NT, C]) for s in (X, Y)]
        agg = [sb(f"agg_{s}", [P, N]) for s in (X, Y)]
        y = [sb(f"y_{s}", [P, NT, C]) for s in (X, Y)]
        yo = [sb(f"yo_{s}", [P, NT, C]) for s in (X, Y)]
        junk = sb("junk", [P, 2, NT, C], BF16)
        ecol = [sb(f"ecol_{s}", [P, 2, NT]) for s in (X, Y)]
        mx = [sb(f"mx_{s}", [P, NT]) for s in (X, Y)]
        nmx = [sb(f"nmx_{s}", [P, NT]) for s in (X, Y)]
        den = [sb(f"den_{s}", [P, NT]) for s in (X, Y)]
        rden = [sb(f"rden_{s}", [P, NT]) for s in (X, Y)]

        norm_key = [("pre", X), ("pre", Y), ("post", X), ("post", Y)]
        stats = {k: sb(f"stats_{k[0]}{k[1]}", [P, NT, 6]) for k in norm_key}
        both = {k: sb(f"both_{k[0]}{k[1]}", [P, NT, 2]) for k in norm_key}
        dif = {k: sb(f"dif_{k[0]}{k[1]}", [P, NT]) for k in norm_key}
        mean = {k: sb(f"mean_{k[0]}{k[1]}", [P, NT]) for k in norm_key}
        ve = {k: sb(f"ve_{k[0]}{k[1]}", [P, NT]) for k in norm_key}
        rstd = {k: sb(f"rstd_{k[0]}{k[1]}", [P, NT]) for k in norm_key}

        b_r, b_z, b_xn, b_hn = bank("b_r"), bank("b_z"), bank("b_xn"), bank("b_hn")
        b_u, b_t = bank("b_u"), bank("b_t")
        b_agg, b_lin = bank("b_agg"), bank("b_lin")

        weights_in = sem("weights_in")
        setup_pool, setup_dve, setup_pe, setup_copied = (
            sem("setup_pool"), sem("setup_dve"), sem("setup_pe"), sem("setup_copied"))
        a_in = [sem(f"a_in_{s}") for s in (X, Y)]
        apre_in, atpre_in = sem("apre_in"), sem("atpre_in")
        x0_in = [sem(f"x0_in_{s}") for s in (X, Y)]
        at_in = [sem(f"at_in_{s}") for s in (X, Y)]
        out_stored = [sem(f"out_stored_{s}") for s in (X, Y)]

        t_done, t_copied = sem("t_done"), sem("t_copied")
        u_done, u_copied = sem("u_done"), sem("u_copied")
        ghn_done, gr_done, gxn_done, gz_done = sem("ghn_done"), sem("gr_done"), sem("gxn_done"), sem("gz_done")
        r_ready, ztanh_ready, z_ready, n_ready = (
            sem("r_ready"), sem("ztanh_ready"), sem("z_ready"), sem("n_ready"))
        t_ready, pre_n_ready, w_ready, h_ready = sem("t_ready"), sem("pre_n_ready"), sem("w_ready"), sem("h_ready")
        zh_ready = sem("zh_ready")

        back_done, back_read = sem("back_done"), sem("back_read")
        res_kept = sem("res_kept")
        x1_ready = sem("x1_ready")
        deg_ready, adiag_ready, dd_ready, ddp_ready = (
            sem("deg_ready"), sem("adiag_ready"), sem("dd_ready"), sem("ddp_ready"))
        atdiag_ready, xs0_ready = sem("atdiag_ready"), sem("xs0_ready")
        x0_used = sem("x0_used")
        agg_done = {k: sem(f"agg_done_{k}") for k in ("l0", "att", "l3")}
        agg_copied = {k: sem(f"agg_copied_{k}") for k in ("l0", "att", "l3")}
        lin_done = {k: sem(f"lin_done_{k}") for k in ("l0", "att", "l3", "bcast")}
        lin_read = {k: sem(f"lin_read_{k}") for k in ("l0", "att", "l3", "bcast")}
        var_ready = {k: sem(f"var_ready_{k}") for k in ("post", "att", "l3", "l0")}
        rstd_ready = {k: sem(f"rstd_ready_{k}") for k in ("post", "att", "l3", "l0")}
        ediag_ready = sem("ediag_ready")
        mask_ready, maskdiag_ready = sem("mask_ready"), sem("maskdiag_ready")
        umax_ready, nmx_ready = sem("umax_ready"), sem("nmx_ready")
        logit_ready, lrelu_ready, exp_ready = sem("logit_ready"), sem("lrelu_ready"), sem("exp_ready")
        xs2_ready, x3_ready, xs3_ready, xb_ready = (
            sem("xs2_ready"), sem("x3_ready"), sem("xs3_ready"), sem("xb_ready"))
        out_ready = sem("out_ready")
        chain_sem = {k: sem(f"dve_chain_{k}") for k in ("pre", "post")}

        block = ctx.enter_context(nc.Block())

        def bodies(eng, body):
            body(0, 0, 0, {"pre"})
            body(1, 0, 0, {"pre", "gru"})
            body(2, 1, 0, {"pre", "gru", "post"})
            with eng.Fori(2, PAIRS - 1) as i:
                body(i + 1, i, i - 1, {"pre", "gru", "post"})
            body(PAIRS, PAIRS - 1, PAIRS - 2, {"gru", "post"})
            body(PAIRS, PAIRS, PAIRS - 1, {"post"})

        flow_of = {"l0": "pre", "att": "post", "l3": "post", "bcast": "post", "post": "post"}

        def tiles(ap):
            return ap.rearrange("p (t c) -> p t c", t=NT)

        def bc(col):
            return col.unsqueeze(2).to_broadcast([P, NT, C])

        def diagonal(m):
            flat = m[:, :, :].rearrange("p t n -> p (t n)")
            return bass.AP(flat.tensor, flat.offset, [list(flat.ap[0]), [N + P, NT], [1, P]])

        @block.sync
        def _(sp):
            for dst, src in ((w1t, w1t_in), (wiht, wiht_in), (whht, whht_in), (bih, bih_in), (bhh, bhh_in),
                             (k0, k0_in), (wpre, wpre_in), (wpret, wpret_in), (avec, avec_in), (w3, w3_in),
                             (nmask, mask_in)):
                sp.dma_start(dst[:], src).then_inc(weights_in, 16)
            sp.dma_start(bias3[:], bias3_in.to_broadcast([P, C])).then_inc(weights_in, 16)

            def body(pre, gru, post, on):
                def load_pre(s):
                    g = 2 * pre + s
                    if not is_first(pre):
                        sp.wait_ge(weights_in, 16 * 12)
                        sp.wait_ge(x0_used, g - 1)
                    if s == Y or not is_first(pre):
                        sp.wait_ge(deg_ready, g)
                        sp.wait_ge(adiag_ready, g)
                    sp.dma_start(x0[s][:], x_in[g]).then_inc(x0_in[s], 16)
                    sp.dma_start(a_pre[:], adj_in[g]).then_inc(apre_in, 16)
                    if s == Y or not is_first(pre):
                        sp.wait_ge(agg_done["l0"], g)
                    sp.dma_start(at_pre[:], adjt_in[g]).then_inc(atpre_in, 16)

                def load_gru(s):
                    if not is_first(gru):
                        sp.wait_ge(u_done, STEPS * (gru - 1) + STEPS - 2 + s + 1)
                    sp.dma_start(a[s][:], adj_in[2 * gru + s]).then_inc(a_in[s], 16)

                def load_post(s):
                    if not is_first(post):
                        sp.wait_ge(agg_done["l3"], 2 * post - 1 + s)
                    sp.dma_start(at[s][:], adjt_in[2 * post + s]).then_inc(at_in[s], 16)

                if "post" in on:
                    load_post(X)
                if "gru" in on:
                    load_gru(X)
                if "post" in on:
                    load_post(Y)
                if "gru" in on:
                    load_gru(Y)
                if "pre" in on:
                    load_pre(X)
                    load_pre(Y)

            def is_first(run):
                return isinstance(run, int) and run == 0

            bodies(sp, body)
            for s in (X, Y):
                sp.wait_ge(out_stored[s], 16 * PAIRS)

        @block.tensor
        def _(pe):
            pe.wait_ge(weights_in, 16 * 12)
            for layer, b in enumerate((b_r, b_z, b_xn, b_hn)):
                nc.tensor.matmul(b[:, 0:G], w1t[:, layer, :], wiht[:, layer, :],
                                 start=True, stop=True).then_inc(setup_pe, 1)
            pe.wait_ge(setup_dve, 1)
            for e in range(2):
                nc.tensor.matmul(b_u[:, e * C:(e + 1) * C], acols[:, e, :], wpret[:],
                                 start=True, stop=True).then_inc(setup_pe, 1)
            pe.wait_ge(setup_copied, L + 1)
            pe.wait_ge(setup_pool, 2)

            def transposes(src, tiled):
                for t in range(NT):
                    part = src[:, t, :] if tiled else src[:, t * P:(t + 1) * P]
                    last = nc.tensor.transpose(b_t[:, t * P:(t + 1) * P], part, ident[:])
                return last

            def body(pre, gru, post, on):
                reading = []
                last_lin = []

                def free_agg():
                    if reading:
                        pe.wait_ge(*reading.pop())

                def free_lin():
                    if last_lin:
                        pe.wait_ge(*last_lin.pop())
                    elif "gru" in on:
                        pe.wait_ge(lin_read["l0"], 2 * pre)
                    elif "post" in on:
                        pe.wait_ge(lin_read["l3"], 2 * post)

                def aggregate(kind, s, run, lhs, rhs):
                    free_agg()
                    for t in range(NT):
                        last = nc.tensor.matmul(b_agg[:], lhs[:, t, :], rhs[:, t, :],
                                                start=(t == 0), stop=(t == NT - 1))
                    last.then_inc(agg_done[kind], 1)
                    reading.append((agg_copied[kind], 2 * run + s + 1))

                def linear(kind, s, run, aggT, w):
                    free_lin()
                    pe.wait_ge(agg_copied[kind], 2 * run + s + 1)
                    for t in range(NT):
                        last = nc.tensor.matmul(b_lin[:, t * C:(t + 1) * C], aggT[:, t * P:(t + 1) * P], w[:],
                                                start=True, stop=True)
                    last.then_inc(lin_done[kind], 1)
                    last_lin.append((lin_read[kind], 2 * run + s + 1))

                def post_back(s):
                    pe.wait_ge(h_ready, STEPS * post + STEPS - 2 + s + 1)
                    if s == Y:
                        if "gru" in on:
                            pe.wait_ge(t_copied, STEPS * gru + 1)
                        pe.wait_ge(back_read, 2 * post + 1)
                    transposes(hT[s], False).then_inc(back_done, 1)

                def att_bcast(s):
                    pe.wait_ge(ediag_ready, 2 * post + s + 1)
                    free_lin()
                    nc.tensor.matmul(b_lin[:], ones[:], es[s][:], start=True, stop=True)\
                        .then_inc(lin_done["bcast"], 1)
                    last_lin.append((lin_read["bcast"], 2 * post + s + 1))

                def att_agg(s):
                    pe.wait_ge(xs2_ready, 2 * post + s + 1)
                    aggregate("att", s, post, xs[s], att[s])

                def att_lin(s):
                    linear("att", s, post, agg[s], wpre)

                def l3_agg(s):
                    pe.wait_ge(at_in[s], 16 * (post + 1))
                    pe.wait_ge(xs3_ready, 2 * post + s + 1)
                    aggregate("l3", s, post, xs[s], at[s])

                def l3_lin(s):
                    linear("l3", s, post, agg[s], w3)

                def l0_agg(s):
                    pe.wait_ge(atdiag_ready, 2 * pre + s + 1)
                    pe.wait_ge(xs0_ready, 2 * pre + s + 1)
                    aggregate("l0", s, pre, xs_pre, at_pre)

                def l0_lin(s):
                    linear("l0", s, pre, agg_pre, k0)

                pieces = dict(post_back=post_back, att_bcast=att_bcast, att_agg=att_agg, att_lin=att_lin,
                              l3_agg=l3_agg, l3_lin=l3_lin, l0_agg=l0_agg, l0_lin=l0_lin)

                def fill(point):
                    for name, s in PE_FILL.get(point, ()):
                        if ("pre" if name.startswith("l0") else "post") in on:
                            pieces[name](s)

                def turn(q):
                    layer, s = divmod(q, 2)
                    if layer == 0:
                        if "post" in on:
                            pe.wait_ge(back_read, 2 * post + s + 1)
                        pe.wait_ge(x1_ready, 2 * gru + s + 1)
                        transposes(x1[s], True).then_inc(t_done, 1)
                    else:
                        pe.wait_ge(h_ready, STEPS * gru + q - 1)
                        transposes(hT[s], False).then_inc(t_done, 1)

                def step(q):
                    layer, s = divmod(q, 2)
                    n = STEPS * gru + q
                    first = q == 0 and isinstance(gru, int) and gru == 0
                    if layer == 0:
                        pe.wait_ge(a_in[s], 16 * (gru + 1))
                        pe.wait_ge(x1_ready, 2 * gru + s + 1)
                        h = x1[s]
                    else:
                        pe.wait_ge(t_copied, n + 1)
                        h = hn[s]
                    for t in range(NT):
                        last = nc.tensor.matmul(b_u[:], h[:, t, :], a[s][:, t, :],
                                                start=(t == 0), stop=(t == NT - 1))
                    last.then_inc(u_done, 1)
                    if q == 0:
                        turn(0)
                    fill(2 * q)
                    if not first:
                        pe.wait_ge(ztanh_ready, n)
                        pe.wait_ge(pre_n_ready, n)
                    if layer == 0:
                        pe.wait_ge(t_copied, n + 1)
                    wx, wh = wg[:, layer, :], whht[:, layer, :]
                    nc.tensor.matmul(b_hn[:], wh[:, 2 * C:3 * C], hT[s][:], start=True, stop=True)\
                        .then_inc(ghn_done, 1)
                    nc.tensor.matmul(b_r[:], wh[:, 0:C], hT[s][:], start=True, stop=False)
                    nc.tensor.matmul(b_z[:], wh[:, C:2 * C], hT[s][:], start=True, stop=False)
                    pe.wait_ge(u_copied, n + 1)
                    nc.tensor.matmul(b_r[:], wx[:, 0:C], uT[s][:], start=False, stop=True).then_inc(gr_done, 1)
                    nc.tensor.matmul(b_xn[:], wx[:, 2 * C:3 * C], uT[s][:], start=True, stop=True)\
                        .then_inc(gxn_done, 1)
                    if q + 1 < STEPS:
                        turn(q + 1)
                    nc.tensor.matmul(b_z[:], wx[:, C:2 * C], uT[s][:], start=False, stop=True)\
                        .then_inc(gz_done, 1)
                    fill(2 * q + 1)

                if "post" in on:
                    post_back(X)
                for q in range(STEPS):
                    if "gru" in on:
                        step(q)
                    else:
                        fill(2 * q)
                        fill(2 * q + 1)

            bodies(pe, body)

        @block.scalar
        def _(act):
            for layer, b in enumerate((b_r, b_z, b_xn, b_hn)):
                act.wait_ge(setup_pe, layer + 1)
                nc.scalar.activation(wg[:, layer, :], b[:, 0:G], ACT.Copy).then_inc(setup_copied, 1)
            act.wait_ge(setup_pe, L + 2)
            nc.scalar.activation(arow[:, :, :].rearrange("p e c -> p (e c)"), b_u[:, 0:2 * C], ACT.Copy)\
                .then_inc(setup_copied, 1)
            act.wait_ge(setup_dve, 2)

            def body(pre, gru, post, on):
                def degree(s):
                    act.wait_ge(apre_in, 16 * (2 * pre + s + 1))
                    if s == Y or not (isinstance(pre, int) and pre == 0):
                        act.wait_ge(dd_ready, 2 * pre + s)
                    for t in range(NT):
                        last = nc.scalar.activation(scratch[:, t, :], a_pre[:, t, :], ACT.Copy,
                                                    accum_out=deg[:, t:t + 1])
                    last.then_inc(deg_ready, 1)

                def agg_copy(kind, s, run, dst):
                    act.wait_ge(agg_done[kind], 2 * run + s + 1)
                    nc.scalar.activation(dst[:], b_agg[:], ACT.Copy).then_inc(agg_copied[kind], 1)

                def agg_l0(s):
                    agg_copy("l0", s, pre, agg_pre)

                def agg_att(s):
                    agg_copy("att", s, post, agg[s])

                def agg_l3(s):
                    agg_copy("l3", s, post, agg[s])

                def att_bcast(s):
                    act.wait_ge(lin_done["bcast"], 2 * post + s + 1)
                    nc.scalar.activation(es[s][:], b_lin[:], ACT.Copy).then_inc(lin_read["bcast"], 1)

                def att_logits(s):
                    g = 2 * post + s
                    for t in range(NT + 1):
                        if t < NT:
                            act.wait_ge(umax_ready, NT * g + t + 1)
                            nc.scalar.activation(att[s][:, t, :], att[s][:, t, :], ACT.Identity,
                                                 bias=ecol[s][:, 1, t:t + 1]).then_inc(logit_ready, 1)
                        if t >= 1:
                            if t == 1:
                                act.wait_ge(nmx_ready, g + 1)
                            act.wait_ge(lrelu_ready, NT * g + t)
                            nc.scalar.activation(att[s][:, t - 1, :], att[s][:, t - 1, :], ACT.Exp,
                                                 bias=nmx[s][:, t - 1:t],
                                                 accum_out=den[s][:, t - 1:t]).then_inc(exp_ready, 1)

                pieces = dict(degree=degree, agg_l0=agg_l0, agg_att=agg_att, agg_l3=agg_l3,
                              att_bcast=att_bcast, att_logits=att_logits)

                def store(s, runs):
                    act.wait_ge(out_ready, 2 * runs - 1 + s)
                    act.dma_start(out[2 * (runs - 1) + s], yo[s][:]).then_inc(out_stored[s], 16)

                def fill(point):
                    for name, s in ACT_FILL.get(point, ()):
                        if ("pre" if name in ("degree", "agg_l0") else "post") in on:
                            pieces[name](s)

                def step(q):
                    layer, s = divmod(q, 2)
                    n = STEPS * gru + q
                    act.wait_ge(u_done, n + 1)
                    nc.scalar.activation(uT[s][:], b_u[:], ACT.Copy).then_inc(u_copied, 1)
                    if q == 0:
                        act.wait_ge(t_done, n + 1)
                        nc.scalar.activation(hT[X][:], b_t[:], ACT.Copy).then_inc(t_copied, 1)
                    fill(2 * q)
                    act.wait_ge(ghn_done, n + 1)
                    nc.scalar.activation(hb[s][:], b_hn[:], ACT.Identity, bias=half_b[:, layer, 2:3], scale=0.5)
                    act.wait_ge(gr_done, n + 1)
                    nc.scalar.activation(rg[s][:], b_r[:], ACT.Tanh, bias=half_b[:, layer, 0:1], scale=0.5)\
                        .then_inc(r_ready, 1)
                    if q + 1 < STEPS:
                        act.wait_ge(t_done, n + 2)
                        dst = hT[Y][:] if q == 0 else hn[1 - s][:, :, :].rearrange("p t c -> p (t c)")
                        nc.scalar.activation(dst, b_t[:], ACT.Copy).then_inc(t_copied, 1)
                    act.wait_ge(gz_done, n + 1)
                    nc.scalar.activation(zg[s][:], b_z[:], ACT.Tanh, bias=half_b[:, layer, 1:2], scale=0.5)\
                        .then_inc(ztanh_ready, 1)
                    act.wait_ge(ztanh_ready, n + 1)
                    nc.scalar.activation(zg[s][:], zg[s][:], ACT.Copy, bias=0.5, scale=0.5)\
                        .then_inc(z_ready, 1)
                    fill(2 * q + 1)
                    act.wait_ge(pre_n_ready, n + 1)
                    nc.scalar.activation(ng[s][:], tg[s][:], ACT.Tanh, bias=bih[:, layer, 2:3])\
                        .then_inc(n_ready, 1)

                for q in range(STEPS):
                    if "gru" in on:
                        step(q)
                    else:
                        fill(2 * q)
                        fill(2 * q + 1)
                    if q == STEPS - 1 and "post" in on:
                        store(X, post + 1)
                        store(Y, post + 1)

            bodies(act, body)

        @block.vector
        def _(dve):
            dve.wait_ge(weights_in, 16 * 12)
            dve.wait_ge(setup_pool, 2)
            for e in range(2):
                last = nc.vector.tensor_scalar(acols[:, e, :], ones[:], avec[:, e:e + 1], None, ALU.mult)
            last.then_inc(setup_dve, 1)
            nc.vector.tensor_tensor(half_b[:, :, 0:2], bih[:, :, 0:2], bhh[:, :, 0:2], ALU.add)
            nc.vector.tensor_copy(half_b[:, :, 2:3], bhh[:, :, 2:3]).then_inc(setup_copied, 1)
            dve.wait_ge(setup_copied, L + 2)
            nc.vector.tensor_scalar(half_b[:], half_b[:], 0.5, None, ALU.mult).then_inc(setup_dve, 1)

            def body(pre, gru, post, on):
                marks = {"pre": 0, "post": 0}
                runs = {"pre": pre, "post": post}

                def link(flow, ins):
                    marks[flow] += 1
                    ins.then_inc(chain_sem[flow], 1)
                    dve.wait_ge(chain_sem[flow], DVE_LINKS[flow] * runs[flow] + marks[flow])

                def own():
                    dve.wait_ge(setup_dve, 1)

                def statistics(kind, s, src):
                    flow = flow_of[kind]
                    k = (flow, s)
                    for t in range(NT):
                        last = nc.vector.bn_stats(stats[k][:, t, :], src[:, t, :])
                    link(flow, last)
                    even, odd = stats[k][:, :, 1:3], stats[k][:, :, 4:6]
                    nc.vector.tensor_tensor(both[k][:], even, odd, ALU.add)
                    link(flow, nc.vector.tensor_tensor(dif[k][:], even[:, :, 0], odd[:, :, 0], ALU.subtract))
                    nc.vector.tensor_scalar(mean[k][:], both[k][:, :, 0], 0.5, None, ALU.mult)
                    nc.vector.tensor_scalar(ve[k][:], both[k][:, :, 1], 1.0 / C, LN_EPS, ALU.mult, ALU.add)
                    link(flow, nc.vector.scalar_tensor_tensor(dif[k][:], dif[k][:], 0.25, dif[k][:],
                                                              ALU.mult, ALU.mult))
                    nc.vector.tensor_tensor(ve[k][:], ve[k][:], dif[k][:], ALU.add)\
                        .then_inc(var_ready[kind], 1)

                def normalise(kind, s, src, dst, ready):
                    k = (flow_of[kind], s)
                    dve.wait_ge(rstd_ready[kind], 2 * runs[flow_of[kind]] + s + 1)
                    for t in range(NT):
                        last = nc.vector.tensor_scalar(dst[:, t, :], src[:, t, :], mean[k][:, t:t + 1],
                                                       rstd[k][:, t:t + 1], ALU.subtract, ALU.mult)
                    if ready is None:
                        link(flow_of[kind], last)
                    else:
                        last.then_inc(ready, 1)

                def post_read(s):
                    g = 2 * post + s
                    dve.wait_ge(back_done, g + 1)
                    m = nmask[:, bass.ds(g, 1), :].rearrange("p b t -> p (b t)")
                    nc.vector.tensor_tensor(y[s][:], tiles(b_t[:]), bc(m), ALU.mult).then_inc(back_read, 1)

                def post_res(s):
                    dve.wait_ge(back_read, 2 * post + s + 1)
                    link("post", nc.vector.tensor_tensor(y[s][:], y[s][:], res[s][:], ALU.add))
                    keep_x1(s)
                    statistics("post", s, y[s])

                def keep_x1(s):
                    if "gru" in on:
                        dve.wait_ge(x1_ready, 2 * gru + s + 1)
                        nc.vector.tensor_copy(res[s][:], x1[s][:]).then_inc(res_kept, 1)

                def norm_post(s):
                    normalise("post", s, y[s], x2[s], None)

                def mask(s):
                    dve.wait_ge(at_in[s], 16 * (post + 1))
                    nc.vector.tensor_scalar(att[s][:], at[s][:], 0.0, MASKED, ALU.is_le, ALU.mult)\
                        .then_inc(mask_ready, 1)

                def att_scores(s):
                    for e in range(2):
                        for t in range(NT):
                            last = nc.vector.tensor_tensor_reduce(
                                out=junk[:, e, t, :], in0=x2[s][:, t, :], in1=arow[:, e, :], scale=1.0, scalar=0.0,
                                op0=ALU.mult, op1=ALU.add, accum_out=ecol[s][:, e, t:t + 1])
                    link("post", last)
                    nc.vector.tensor_tensor(tiles(es[s][:]), ident[:].unsqueeze(1).to_broadcast([P, NT, P]),
                                            bc(ecol[s][:, 0, :]), ALU.mult).then_inc(ediag_ready, 1)

                def att_max(s):
                    g = 2 * post + s
                    own()
                    dve.wait_ge(lin_read["bcast"], g + 1)
                    dve.wait_ge(maskdiag_ready, g + 1)
                    for t in range(NT):
                        last = nc.vector.tensor_tensor_reduce(
                            out=att[s][:, t, :], in0=att[s][:, t, :], in1=es[s][:], scale=1.0, scalar=-3e38,
                            op0=ALU.add, op1=ALU.max, accum_out=mx[s][:, t:t + 1])
                        last.then_inc(umax_ready, 1)
                    dve.wait_ge(umax_ready, NT * g + NT)
                    link("post", nc.vector.tensor_tensor(mx[s][:], mx[s][:], ecol[s][:, 1, :], ALU.add))
                    link("post", nc.vector.scalar_tensor_tensor(mx[s][:], mx[s][:], SLOPE, mx[s][:],
                                                                ALU.mult, ALU.max))
                    nc.vector.tensor_scalar(nmx[s][:], mx[s][:], -1.0, None, ALU.mult).then_inc(nmx_ready, 1)

                def att_lrelu(s):
                    g = 2 * post + s
                    for t in range(NT):
                        dve.wait_ge(logit_ready, NT * g + t + 1)
                        nc.vector.scalar_tensor_tensor(att[s][:, t, :], att[s][:, t, :], SLOPE, att[s][:, t, :],
                                                       ALU.mult, ALU.max).then_inc(lrelu_ready, 1)

                def att_weight(s):
                    dve.wait_ge(exp_ready, NT * (2 * post + s + 1))
                    link("post", nc.vector.reciprocal(rden[s][:], den[s][:]))
                    nc.vector.tensor_tensor(xs[s][:], x2[s][:], bc(rden[s][:]), ALU.mult).then_inc(xs2_ready, 1)

                def att_res(s):
                    dve.wait_ge(lin_done["att"], 2 * post + s + 1)
                    nc.vector.tensor_tensor(y[s][:], tiles(b_lin[:]), x2[s][:], ALU.add)\
                        .then_inc(lin_read["att"], 1)
                    dve.wait_ge(lin_read["att"], 2 * post + s + 1)
                    statistics("att", s, y[s])

                def norm_att(s):
                    normalise("att", s, y[s], x3[s], x3_ready)
                    dve.wait_ge(x3_ready, 2 * post + s + 1)
                    nc.vector.tensor_tensor(xs[s][:], x3[s][:], bc(d3_post[:, s, :]), ALU.mult)\
                        .then_inc(xs3_ready, 1)

                def l3_res(s):
                    g = 2 * post + s
                    dve.wait_ge(lin_done["l3"], g + 1)
                    nc.vector.tensor_tensor(y[s][:], tiles(b_lin[:]), bc(d3_post[:, s, :]), ALU.mult)\
                        .then_inc(lin_read["l3"], 1)
                    dve.wait_ge(lin_read["l3"], g + 1)
                    dve.wait_ge(xb_ready, g + 1)
                    link("post", nc.vector.tensor_tensor(y[s][:], y[s][:], x3[s][:], ALU.add))
                    statistics("l3", s, y[s])

                def norm_l3(s):
                    if not (isinstance(post, int) and post == 0):
                        dve.wait_ge(out_stored[s], 16 * post)
                    normalise("l3", s, y[s], yo[s], out_ready)

                def l0_degree(s):
                    g = 2 * pre + s
                    dve.wait_ge(adiag_ready, g + 1)
                    link("pre", nc.vector.reduce_sum(ann[:], adiag[:], AX_X))
                    dve.wait_ge(deg_ready, g + 1)
                    link("pre", nc.vector.tensor_tensor(ann[:], deg[:], ann[:], ALU.subtract))
                    nc.vector.tensor_scalar(dd[:, 0:NT], ann[:], 1.0, None, ALU.add)
                    nc.vector.tensor_scalar(dd[:, NT:2 * NT], deg[:], DEG_EPS, None, ALU.add)\
                        .then_inc(dd_ready, 1)

                def l0_scale(s):
                    g = 2 * pre + s
                    dve.wait_ge(ddp_ready, g + 1)
                    link("pre", nc.vector.tensor_scalar(d0[:], ddp[:, 0:NT], DEG_EPS, None, ALU.add))
                    link("pre", nc.vector.reciprocal(d0[:], d0[:]))
                    nc.vector.tensor_copy(d3_pre[:, s, :], ddp[:, NT:2 * NT])
                    dve.wait_ge(x0_in[s], 16 * (pre + 1))
                    if s == Y or not (isinstance(pre, int) and pre == 0):
                        dve.wait_ge(agg_done["l0"], g)
                    nc.vector.tensor_tensor(xs_pre[:], x0[s][:], bc(d0[:]), ALU.mult).then_inc(xs0_ready, 1)

                def l0_res(s):
                    g = 2 * pre + s
                    dve.wait_ge(lin_done["l0"], g + 1)
                    nc.vector.tensor_tensor(y_pre[:], tiles(b_lin[:]), bc(d0[:]), ALU.mult)\
                        .then_inc(lin_read["l0"], 1)
                    dve.wait_ge(lin_read["l0"], g + 1)
                    nc.vector.scalar_tensor_tensor(y_pre[:], y_pre[:], 0.0, x0[s][:], ALU.max, ALU.add)\
                        .then_inc(x0_used, 1)
                    dve.wait_ge(x0_used, g + 1)
                    statistics("l0", s, y_pre)

                def norm_l0(s):
                    if "gru" in on:
                        dve.wait_ge(t_done, STEPS * gru + s + 1)
                        dve.wait_ge(res_kept, 2 * gru + s + 1)
                    normalise("l0", s, y_pre, x1[s], x1_ready)

                pieces = dict(post_read=post_read, post_res=post_res, norm_post=norm_post, mask=mask, att_scores=att_scores,
                              att_max=att_max, att_lrelu=att_lrelu, att_weight=att_weight, att_res=att_res,
                              norm_att=norm_att, l3_res=l3_res, norm_l3=norm_l3, l0_degree=l0_degree,
                              l0_scale=l0_scale, l0_res=l0_res, norm_l0=norm_l0)
                of_pre = ("l0_degree", "l0_scale", "l0_res", "norm_l0")

                def fill(point):
                    for name, s in DVE_FILL.get(point, ()):
                        if ("pre" if name in of_pre else "post") in on:
                            pieces[name](s)
                        elif name == "post_res" and "gru" in on:
                            keep_x1(s)

                def step(q):
                    s = q % 2
                    n = STEPS * gru + q
                    fill(2 * q)
                    dve.wait_ge(r_ready, n + 1)
                    nc.vector.scalar_tensor_tensor(tg[s][:], rg[s][:], 1.0, hb[s][:], ALU.add, ALU.mult)\
                        .then_inc(t_ready, 1)
                    dve.wait_ge(gxn_done, n + 1)
                    dve.wait_ge(t_ready, n + 1)
                    nc.vector.tensor_tensor(tg[s][:], b_xn[:], tg[s][:], ALU.add).then_inc(pre_n_ready, 1)
                    fill(2 * q + 1)
                    dve.wait_ge(n_ready, n + 1)
                    nc.vector.scalar_tensor_tensor(ng[s][:], zg[s][:], 1.0, ng[s][:], ALU.subtract, ALU.mult)\
                        .then_inc(w_ready, 1)
                    dve.wait_ge(w_ready, n + 1)
                    dve.wait_ge(zh_ready, n + 1)
                    nc.vector.tensor_tensor(hT[s][:], zh[s][:], ng[s][:], ALU.subtract).then_inc(h_ready, 1)

                if "post" in on:
                    link("post", nc.vector.tensor_copy(d3_post[:], d3_gru[:]))
                if "gru" in on:
                    nc.vector.tensor_copy(d3_gru[:], d3_pre[:])
                for q in range(STEPS):
                    if "gru" in on:
                        step(q)
                    else:
                        fill(2 * q)
                        fill(2 * q + 1)
                for flow in ("pre", "post"):
                    assert flow not in on or marks[flow] == DVE_LINKS[flow], (flow, marks[flow])

            bodies(dve, body)

        @block.gpsimd
        def _(pool):
            nc.gpsimd.memset(ones[:], 1.0).then_inc(setup_pool, 1)
            pool.wait_ge(setup_pool, 1)
            nc.gpsimd.affine_select(out=ident[:], in_=ones[:], compare_op=ALU.is_equal, fill=0.0, base=0,
                                    pattern=[[-1, P]], channel_multiplier=1).then_inc(setup_pool, 1)
            nc.gpsimd.memset(exps[:, 0:NT], 0.5).then_inc(setup_pool, 1)
            nc.gpsimd.memset(exps[:, NT:2 * NT], -0.5).then_inc(setup_pool, 1)
            pool.wait_ge(weights_in, 16 * 12)
            pool.wait_ge(setup_pool, 4)

            def body(pre, gru, post, on):
                runs = {"pre": pre, "post": post}

                def one_diagonal(m, value, ready):
                    d = diagonal(m)
                    nc.gpsimd.affine_select(out=d, in_=d, compare_op=ALU.not_equal, fill=value, base=0,
                                            pattern=[[0, NT], [-1, P]], channel_multiplier=1).then_inc(ready, 1)

                def own():
                    pool.wait_ge(setup_pool, 4)

                def diag_a(s):
                    pool.wait_ge(apre_in, 16 * (2 * pre + s + 1))
                    if s == Y or not (isinstance(pre, int) and pre == 0):
                        pool.wait_ge(dd_ready, 2 * pre + s)
                    nc.gpsimd.tensor_tensor(adiag[:], diagonal(a_pre), ident[:].unsqueeze(1)
                                            .to_broadcast([P, NT, P]), ALU.mult).then_inc(adiag_ready, 1)

                def diag_at(s):
                    own()
                    pool.wait_ge(atpre_in, 16 * (2 * pre + s + 1))
                    one_diagonal(at_pre, 1.0, atdiag_ready)

                def powers(s):
                    pool.wait_ge(dd_ready, 2 * pre + s + 1)
                    nc.gpsimd.tensor_tensor(ddp[:], dd[:], exps[:], ALU.pow).then_inc(ddp_ready, 1)

                def mask_diag(s):
                    own()
                    pool.wait_ge(mask_ready, 2 * post + s + 1)
                    one_diagonal(att[s], 0.0, maskdiag_ready)

                def add_bias(s):
                    pool.wait_ge(xs3_ready, 2 * post + s + 1)
                    nc.gpsimd.tensor_tensor(x3[s][:], x3[s][:], bias3[:].unsqueeze(1)
                                            .to_broadcast([P, NT, C]), ALU.add).then_inc(xb_ready, 1)

                def rstd_of(kind):
                    flow = flow_of[kind]

                    def piece(s):
                        pool.wait_ge(var_ready[kind], 2 * runs[flow] + s + 1)
                        nc.gpsimd.tensor_tensor(rstd[flow, s][:], ve[flow, s][:], exps[:, NT:2 * NT], ALU.pow)\
                            .then_inc(rstd_ready[kind], 1)
                    return piece

                pieces = dict(diag_a=diag_a, diag_at=diag_at, powers=powers, mask_diag=mask_diag,
                              add_bias=add_bias, **{f"rstd_{k}": rstd_of(k) for k in ("post", "att", "l3", "l0")})
                of_pre = ("diag_a", "diag_at", "powers", "rstd_l0")

                def fill(point):
                    for name, s in POOL_FILL.get(point, ()):
                        if ("pre" if name in of_pre else "post") in on:
                            pieces[name](s)

                for q in range(STEPS):
                    fill(2 * q)
                    if "gru" in on:
                        n, s = STEPS * gru + q, q % 2
                        pool.wait_ge(z_ready, n + 1)
                        nc.gpsimd.tensor_tensor(zh[s][:], zg[s][:], hT[s][:], ALU.mult).then_inc(zh_ready, 1)
                    fill(2 * q + 1)

            bodies(pool, body)


def kernel(x, adj, nodemask, L0_gnn_kernel, L1_gnn_weight, L1_gnn_w_ih, L1_gnn_w_hh, L1_gnn_b_ih, L1_gnn_b_hh,
           L2_gnn_W_pre, L2_gnn_a_snd, L2_gnn_a_rec, L3_gnn_weight, L3_gnn_bias):
    import numpy as np
    import concourse.bacc as bacc
    from concourse import mybir as mb
    from concourse.bass_utils import run_bass_kernel_spmd as run

    x, adj = np.asarray(x), np.asarray(adj)
    B, N, C = x.shape
    P = 128
    NT = N // P

    def tiled(m):
        return m.reshape(B, NT, P, m.shape[-1]).transpose(0, 2, 1, 3)

    L = np.asarray(L1_gnn_weight).shape[0]
    arrays = {
        "x": tiled(x),
        "adj": tiled(adj),
        "adjt": tiled(adj.transpose(0, 2, 1)),
        "nodemask": np.asarray(nodemask).reshape(B, NT, P).transpose(2, 0, 1),
        "k0": np.asarray(L0_gnn_kernel),
        "w1t": np.asarray(L1_gnn_weight).transpose(2, 0, 1),
        "wiht": np.asarray(L1_gnn_w_ih).transpose(2, 0, 1),
        "whht": np.asarray(L1_gnn_w_hh).transpose(2, 0, 1),
        "bih": np.asarray(L1_gnn_b_ih).reshape(L, 3, C).transpose(2, 0, 1),
        "bhh": np.asarray(L1_gnn_b_hh).reshape(L, 3, C).transpose(2, 0, 1),
        "wpre": np.asarray(L2_gnn_W_pre),
        "wpret": np.asarray(L2_gnn_W_pre).T,
        "avec": np.stack([np.asarray(L2_gnn_a_snd), np.asarray(L2_gnn_a_rec)], axis=1),
        "w3": np.asarray(L3_gnn_weight),
        "bias3": np.asarray(L3_gnn_bias).reshape(1, C),
    }
    arrays = {f"in_{k}": np.ascontiguousarray(v) for k, v in arrays.items()}
    nc = bacc.Bacc("TRN2", target_bir_lowering=False, num_devices=1)
    ins = [nc.dram_tensor(k, v.shape, mb.dt.from_np(v.dtype), kind="ExternalInput").ap() for k, v in arrays.items()]
    out = nc.dram_tensor("out", (B, P, NT, C), mb.dt.float32, kind="ExternalOutput").ap()
    gnn_kernel(nc, *ins, out)
    got = run(nc, [arrays], core_ids=[0]).results[0]["out"]
    return np.ascontiguousarray(got.transpose(0, 2, 1, 3).reshape(B, N, C))
```

```python
from contextlib import ExitStack

import concourse.bass as bass
from concourse import mybir

ALU = mybir.AluOpType
ACT = mybir.ActivationFunctionType
F32 = mybir.dt.float32
F32R = mybir.dt.float32r
BF16 = mybir.dt.bfloat16
AX_X = mybir.AxisListType.X

P = 128
MASKED = -1e30
LN_EPS = 1e-5
DEG_EPS = 1e-6
SLOPE = 0.2

SETUP_STEP = 5

X, Y = 0, 1

PE_FILL = {
    0: [("post_back", Y)],
    4: [("att_bcast", X)],
    7: [("att_bcast", Y)],
    9: [("att_agg", X)],
    10: [("l0_agg", X), ("att_lin", X)],
    13: [("l3_agg", X), ("l0_lin", X)],
    15: [("l3_lin", X), ("att_agg", Y)],
    16: [("l0_agg", Y), ("att_lin", Y)],
    19: [("l0_lin", Y), ("l3_agg", Y)],
    21: [("l3_lin", Y)],
}
ACT_FILL = {
    2: [("degree", X)],
    6: [("att_bcast", X)],
    7: [("att_er", X), ("att_exp", X)],
    8: [("degree", Y), ("att_bcast", Y)],
    9: [("att_er", Y), ("agg_att", X)],
    11: [("agg_l0", X), ("att_exp", Y)],
    14: [("agg_l3", X)],
    15: [("agg_att", Y)],
    16: [("agg_l0", Y)],
    17: [("split_x1", X)],
    19: [("store", X)],
    20: [("split_a", X), ("agg_l3", Y)],
    21: [("split_a", Y)],
    22: [("split_x1", Y)],
    23: [("store", Y)],
}
DVE_FILL = {
    -1: [("post_read", X)],
    0: [("post_res", X), ("post_read", Y), ("mask", X), ("post_res", Y)],
    1: [("norm_post", X)],
    3: [("att_scores", X)],
    4: [("l0_degree", X), ("norm_post", Y)],
    5: [("mask", Y)],
    6: [("att_max", X), ("att_scores", Y)],
    7: [("att_lrelu", X), ("att_weight", X)],
    8: [("l0_scale", X)],
    9: [("att_max", Y), ("att_lrelu", Y)],
    10: [("l0_degree", Y)],
    11: [("att_res", X)],
    12: [("norm_att", X), ("att_weight", Y)],
    13: [("l0_res", X)],
    14: [("norm_l0", X), ("l0_scale", Y)],
    16: [("l3_res", X), ("att_res", Y)],
    18: [("norm_att", Y), ("split_x1", X), ("norm_l3", X)],
    20: [("l0_res", Y)],
    21: [("l3_res", Y), ("norm_l0", Y)],
    22: [("split_x1", Y)],
    23: [("norm_l3", Y)],
}
POOL_FILL = {
    0: [("rstd_post", X), ("diag_a", X)],
    2: [("mask_diag", X), ("rstd_post", Y)],
    5: [("mask_diag", Y)],
    6: [("diag_at", X)],
    7: [("powers", X), ("diag_a", Y)],
    11: [("rstd_att", X), ("powers", Y)],
    12: [("diag_at", Y)],
    14: [("add_bias", X), ("rstd_l0", X)],
    15: [("rstd_l3", X)],
    16: [("rstd_att", Y)],
    17: [("add_bias", Y)],
    19: [("split_a", X)],
    20: [("rstd_l0", Y)],
    21: [("rstd_l3", Y)],
    23: [("split_a", Y)],
}


def gnn_kernel(nc, x_in, adj_in, adjt_in, mask_in, k0_in, w1t_in, wiht_in, whht_in, bih_in, bhh_in,
               wpre_in, wpret_in, avec_in, w3_in, bias3_in, out):
    B, _, NT, C = x_in.shape
    N = NT * P
    L = w1t_in.shape[1]
    PAIRS = B // 2
    G = 3 * C
    STEPS = 2 * L
    DVE_LINKS = {"pre": 14, "post": 33}

    with ExitStack() as ctx:
        def sb(name, shape, dtype=F32):
            return ctx.enter_context(nc.sbuf_tensor(name, shape, dtype))

        def bank(name):
            return ctx.enter_context(nc.psum_tensor(name, [P, N], F32))

        def sem(name):
            return ctx.enter_context(nc.semaphore(name))

        ident = sb("ident", [P, P])
        ones = sb("ones", [P, P])
        wg_hi = sb("wg_hi", [P, L, G], F32R)
        wg_lo = sb("wg_lo", [P, L, G], F32R)
        wh_hi = sb("wh_hi", [P, L, G], F32R)
        wh_lo = sb("wh_lo", [P, L, G], F32R)
        bih = sb("bih", [P, L, 3])
        bhh = sb("bhh", [P, L, 3])
        half_b = sb("half_b", [P, L, 3])
        k0 = sb("k0", [P, C])
        wpre = sb("wpre", [P, C])
        w3 = sb("w3", [P, C])
        avec = sb("avec", [P, 2])
        arow = sb("arow", [P, 2, C])
        bias3 = sb("bias3", [P, C])
        nmask = sb("nmask", [P, B, NT])
        exps = sb("exps", [P, 2 * NT])

        a_raw = [sb(f"a_raw_{s}", [P, NT, N]) for s in (X, Y)]
        at_pre = sb("at_pre", [P, NT, N])
        scratch = sb("scratch", [P, NT, N], BF16)
        x0 = [sb(f"x0_{s}", [P, NT, C]) for s in (X, Y)]
        xs_pre = sb("xs_pre", [P, NT, C])
        adiag = sb("adiag", [P, NT, P])
        y_pre = xs_pre
        agg_pre = sb("agg_pre", [P, N])
        x1 = [sb(f"x1_{s}", [P, NT, C]) for s in (X, Y)]
        deg = sb("deg", [P, NT])
        ann = sb("ann", [P, NT])
        dd = sb("dd", [P, 2 * NT])
        ddp = sb("ddp", [P, 2 * NT])
        d0 = sb("d0", [P, NT])
        d3_pre = sb("d3_pre", [P, 2, NT])
        d3_gru = sb("d3_gru", [P, 2, NT])
        d3_post = sb("d3_post", [P, 2, NT])

        a_hi = [sb(f"a_hi_{s}", [P, NT, N], F32R) for s in (X, Y)]
        a_lo = [sb(f"a_lo_{s}", [P, NT, N], F32R) for s in (X, Y)]
        hT = [sb(f"hT_{s}", [P, N]) for s in (X, Y)]
        hT_hi = [sb(f"hT_hi_{s}", [P, N], F32R) for s in (X, Y)]
        hT_lo = [sb(f"hT_lo_{s}", [P, N], F32R) for s in (X, Y)]
        hn_hi = [sb(f"hn_hi_{s}", [P, NT, C], F32R) for s in (X, Y)]
        hn_lo = [sb(f"hn_lo_{s}", [P, NT, C], F32R) for s in (X, Y)]
        uT_hi = [sb(f"uT_hi_{s}", [P, N], F32R) for s in (X, Y)]
        uT_lo = [sb(f"uT_lo_{s}", [P, N], F32R) for s in (X, Y)]
        rg = [sb(f"rg_{s}", [P, N]) for s in (X, Y)]
        zg = [sb(f"zg_{s}", [P, N]) for s in (X, Y)]
        hb = [sb(f"hb_{s}", [P, N]) for s in (X, Y)]
        ng = [sb(f"ng_{s}", [P, N]) for s in (X, Y)]
        zh = [sb(f"zh_{s}", [P, N]) for s in (X, Y)]

        at = [sb(f"at_{s}", [P, NT, N]) for s in (X, Y)]
        att = [sb(f"att_{s}", [P, NT, N]) for s in (X, Y)]
        es = [sb(f"es_{s}", [P, N]) for s in (X, Y)]
        res = [sb(f"res_{s}", [P, NT, C]) for s in (X, Y)]
        x2 = [sb(f"x2_{s}", [P, NT, C]) for s in (X, Y)]
        x3 = [sb(f"x3_{s}", [P, NT, C]) for s in (X, Y)]
        xs = [sb(f"xs_{s}", [P, NT, C]) for s in (X, Y)]
        agg = [sb(f"agg_{s}", [P, N]) for s in (X, Y)]
        ecol = [sb(f"ecol_{s}", [P, 2, NT]) for s in (X, Y)]
        mx = [sb(f"mx_{s}", [P, NT]) for s in (X, Y)]
        nmx = [sb(f"nmx_{s}", [P, NT]) for s in (X, Y)]
        den = [sb(f"den_{s}", [P, NT]) for s in (X, Y)]
        rden = [sb(f"rden_{s}", [P, NT]) for s in (X, Y)]

        wiht, whht = att[X][:, :, 0:G], att[Y][:, :, 0:G]
        w1t = es[X][:, :].rearrange("p (l c) -> p l c", l=L)
        wpret = es[Y][:, 0:C]
        acols = es[Y][:, C:3 * C].rearrange("p (e c) -> p e c", e=2)

        norm_key = [("pre", X), ("pre", Y), ("post", X), ("post", Y)]
        stats = sb("stats", [P, NT, 6])
        both = {k: sb(f"both_{k[0]}{k[1]}", [P, NT, 2]) for k in norm_key}
        dif = {k: sb(f"dif_{k[0]}{k[1]}", [P, NT]) for k in norm_key}
        mean = {k: sb(f"mean_{k[0]}{k[1]}", [P, NT]) for k in norm_key}
        ve = {k: sb(f"ve_{k[0]}{k[1]}", [P, NT]) for k in norm_key}
        rstd = {k: sb(f"rstd_{k[0]}{k[1]}", [P, NT]) for k in norm_key}

        b_r, b_z, b_xn, b_hn = bank("b_r"), bank("b_z"), bank("b_xn"), bank("b_hn")
        b_u, b_t = bank("b_u"), bank("b_t")
        b_agg, b_lin = bank("b_agg"), bank("b_lin")
        back_bank = (b_agg, b_lin)

        weights_in, k0_loaded = sem("weights_in"), sem("k0_loaded")
        setup_pool, setup_dve, setup_pe, setup_act, setup_copied = (
            sem("setup_pool"), sem("setup_dve"), sem("setup_pe"), sem("setup_act"), sem("setup_copied"))
        araw_in = [sem(f"araw_in_{s}") for s in (X, Y)]
        atpre_in = sem("atpre_in")
        x0_in = [sem(f"x0_in_{s}") for s in (X, Y)]
        at_in = [sem(f"at_in_{s}") for s in (X, Y)]
        out_stored = [sem(f"out_stored_{s}") for s in (X, Y)]

        t_done, xT_copied = sem("t_done"), sem("xT_copied")
        hn_hi_ready, hn_lo_ready = sem("hn_hi_ready"), sem("hn_lo_ready")
        hT_hi_ready, hT_lo_ready = sem("hT_hi_ready"), sem("hT_lo_ready")
        a_hi_ready = [sem(f"a_hi_ready_{s}") for s in (X, Y)]
        a_lo_ready = [sem(f"a_lo_ready_{s}") for s in (X, Y)]
        x1_hi_ready, x1_lo_ready = sem("x1_hi_ready"), sem("x1_lo_ready")
        u_done, u_hi_ready, u_lo_ready = sem("u_done"), sem("u_hi_ready"), sem("u_lo_ready")
        ghn_done, gr_done, gxn_done, gz_done = sem("ghn_done"), sem("gr_done"), sem("gxn_done"), sem("gz_done")
        r_ready, ztanh_ready, z_ready, n_ready = (
            sem("r_ready"), sem("ztanh_ready"), sem("z_ready"), sem("n_ready"))
        t_ready, pre_n_ready, w_ready, h_ready = sem("t_ready"), sem("pre_n_ready"), sem("w_ready"), sem("h_ready")
        zh_ready = sem("zh_ready")

        back_done, back_read = sem("back_done"), sem("back_read")
        res_kept = sem("res_kept")
        x1_ready = sem("x1_ready")
        deg_ready, adiag_ready, dd_ready, ddp_ready = (
            sem("deg_ready"), sem("adiag_ready"), sem("dd_ready"), sem("ddp_ready"))
        atdiag_ready, xs0_ready = sem("atdiag_ready"), sem("xs0_ready")
        x0_used = sem("x0_used")
        agg_done = {k: sem(f"agg_done_{k}") for k in ("l0", "att", "l3")}
        agg_copied = {k: sem(f"agg_copied_{k}") for k in ("l0", "att", "l3")}
        lin_done = {k: sem(f"lin_done_{k}") for k in ("l0", "att", "l3", "bcast")}
        lin_read = {k: sem(f"lin_read_{k}") for k in ("l0", "att", "l3", "bcast")}
        var_ready = {k: sem(f"var_ready_{k}") for k in ("post", "att", "l3", "l0")}
        rstd_ready = {k: sem(f"rstd_ready_{k}") for k in ("post", "att", "l3", "l0")}
        ediag_ready = sem("ediag_ready")
        mask_ready, maskdiag_ready = sem("mask_ready"), sem("maskdiag_ready")
        umax_ready, nmx_ready = sem("umax_ready"), sem("nmx_ready")
        logit_ready, lrelu_ready, exp_ready = sem("logit_ready"), sem("lrelu_ready"), sem("exp_ready")
        xs2_ready, x3_ready, xs3_ready, xb_ready = (
            sem("xs2_ready"), sem("x3_ready"), sem("xs3_ready"), sem("xb_ready"))
        out_ready = sem("out_ready")
        chain_sem = {k: sem(f"dve_chain_{k}") for k in ("pre", "post")}

        block = ctx.enter_context(nc.Block())

        def bodies(eng, body):
            body(0, 0, 0, {"pre", "setup"})
            body(1, 0, 0, {"pre", "gru"})
            body(2, 1, 0, {"pre", "gru", "post"})
            with eng.Fori(2, PAIRS - 1) as i:
                body(i + 1, i, i - 1, {"pre", "gru", "post"})
            body(PAIRS, PAIRS - 1, PAIRS - 2, {"gru", "post"})
            body(PAIRS, PAIRS, PAIRS - 1, {"post"})

        flow_of = {"l0": "pre", "att": "post", "l3": "post", "bcast": "post", "post": "post"}

        def tiles(ap):
            return ap.rearrange("p (t c) -> p t c", t=NT)

        def bc(col):
            return col.unsqueeze(2).to_broadcast([P, NT, C])

        def diagonal(m):
            flat = m[:, :, :].rearrange("p t n -> p (t n)")
            return bass.AP(flat.tensor, flat.offset, [list(flat.ap[0]), [N + P, NT], [1, P]])

        @block.sync
        def _(sp):
            def body(pre, gru, post, on):
                def load_pre(s):
                    g = 2 * pre + s
                    if not is_first(pre):
                        sp.wait_ge(weights_in, 16 * 11)
                        sp.wait_ge(a_lo_ready[s], NT * pre)
                    sp.dma_start(a_raw[s][:], adj_in[g]).then_inc(araw_in[s], 16)
                    if not is_first(pre):
                        sp.wait_ge(weights_in, 16 * 11)
                        sp.wait_ge(x0_used, g - 1)
                    sp.dma_start(x0[s][:], x_in[g]).then_inc(x0_in[s], 16)
                    if "setup" in on and s == X:
                        sp.dma_start(k0[:], k0_in).then_inc(k0_loaded, 16)
                    if "setup" in on and s == Y:
                        load_weights()
                    if s == Y or not is_first(pre):
                        sp.wait_ge(agg_done["l0"], g)
                    sp.dma_start(at_pre[:], adjt_in[g]).then_inc(atpre_in, 16)

                def load_weights():
                    for dst, src in ((w1t, w1t_in), (wiht, wiht_in), (whht, whht_in), (wpret, wpret_in),
                                     (avec[:], avec_in), (bih[:], bih_in), (bhh[:], bhh_in),
                                     (wpre[:], wpre_in), (w3[:], w3_in), (nmask[:], mask_in),
                                     (bias3[:], bias3_in.to_broadcast([P, C]))):
                        sp.dma_start(dst, src).then_inc(weights_in, 16)

                def load_post(s):
                    if not is_first(post):
                        sp.wait_ge(weights_in, 16 * 11)
                        sp.wait_ge(agg_done["l3"], 2 * post - 1 + s)
                    sp.dma_start(at[s][:], adjt_in[2 * post + s]).then_inc(at_in[s], 16)

                if "post" in on:
                    load_post(X)
                if "pre" in on:
                    load_pre(X)
                if "post" in on:
                    load_post(Y)
                if "pre" in on:
                    load_pre(Y)

            def is_first(run):
                return isinstance(run, int) and run == 0

            bodies(sp, body)
            for s in (X, Y):
                sp.wait_ge(out_stored[s], 16 * PAIRS)

        @block.tensor
        def _(pe):
            def setup():
                pe.wait_ge(weights_in, 16 * 11)
                for layer, b in enumerate((b_r, b_z, b_xn, b_hn)):
                    nc.tensor.matmul(b[:, 0:G], w1t[:, layer, :], wiht[:, layer, :],
                                     start=True, stop=True).then_inc(setup_pe, 1)
                pe.wait_ge(setup_dve, 1)
                for e in range(2):
                    nc.tensor.matmul(b_u[:, e * C:(e + 1) * C], acols[:, e, :], wpret,
                                     start=True, stop=True).then_inc(setup_pe, 1)
                pe.wait_ge(setup_copied, L + 2)
                pe.wait_ge(setup_pool, 2)

            def transposes(bank, src, tiled):
                for t in range(NT):
                    part = src[:, t, :] if tiled else src[:, t * P:(t + 1) * P]
                    last = nc.tensor.transpose(bank[:, t * P:(t + 1) * P], part, ident[:])
                return last

            def body(pre, gru, post, on):
                last_agg, last_lin = [], []

                def free(last, read):
                    if last:
                        pe.wait_ge(*last.pop())
                    else:
                        if not (isinstance(pre, int) and pre == 0):
                            pe.wait_ge(read["l0"], 2 * pre)
                        if not (isinstance(post, int) and post == 0):
                            pe.wait_ge(read["l3"], 2 * post)

                def free_agg():
                    free(last_agg, agg_copied)

                def free_lin():
                    free(last_lin, lin_read)

                def aggregate(kind, s, run, lhs, rhs):
                    free_agg()
                    for t in range(NT):
                        last = nc.tensor.matmul(b_agg[:], lhs[:, t, :], rhs[:, t, :],
                                                start=(t == 0), stop=(t == NT - 1))
                    last.then_inc(agg_done[kind], 1)
                    last_agg.append((agg_copied[kind], 2 * run + s + 1))

                def linear(kind, s, run, aggT, w):
                    free_lin()
                    pe.wait_ge(agg_copied[kind], 2 * run + s + 1)
                    for t in range(NT):
                        last = nc.tensor.matmul(b_lin[:, t * C:(t + 1) * C], aggT[:, t * P:(t + 1) * P], w[:],
                                                start=True, stop=True)
                    last.then_inc(lin_done[kind], 1)
                    last_lin.append((lin_read[kind], 2 * run + s + 1))

                def post_back(s):
                    pe.wait_ge(h_ready, STEPS * post + STEPS - 2 + s + 1)
                    free_agg() if s == X else free_lin()
                    transposes(back_bank[s], hT[s], False).then_inc(back_done, 1)
                    (last_agg if s == X else last_lin).append((back_read, 2 * post + s + 1))

                def att_bcast(s):
                    pe.wait_ge(ediag_ready, 2 * post + s + 1)
                    free_lin()
                    nc.tensor.matmul(b_lin[:], ones[:], es[s][:], start=True, stop=True)\
                        .then_inc(lin_done["bcast"], 1)
                    last_lin.append((lin_read["bcast"], 2 * post + s + 1))

                def att_agg(s):
                    pe.wait_ge(xs2_ready, 2 * post + s + 1)
                    aggregate("att", s, post, xs[s], att[s])

                def att_lin(s):
                    linear("att", s, post, agg[s], wpre)

                def l3_agg(s):
                    pe.wait_ge(at_in[s], 16 * (post + 1))
                    pe.wait_ge(xs3_ready, 2 * post + s + 1)
                    aggregate("l3", s, post, xs[s], at[s])

                def l3_lin(s):
                    linear("l3", s, post, agg[s], w3)

                def l0_agg(s):
                    pe.wait_ge(atdiag_ready, 2 * pre + s + 1)
                    pe.wait_ge(xs0_ready, 2 * pre + s + 1)
                    aggregate("l0", s, pre, xs_pre, at_pre)

                def l0_lin(s):
                    if "setup" in on:
                        pe.wait_ge(k0_loaded, 16)
                    linear("l0", s, pre, agg_pre, k0)

                pieces = dict(post_back=post_back, att_bcast=att_bcast, att_agg=att_agg, att_lin=att_lin,
                              l3_agg=l3_agg, l3_lin=l3_lin, l0_agg=l0_agg, l0_lin=l0_lin)

                def fill(point):
                    for name, s in PE_FILL.get(point, ()):
                        if ("pre" if name.startswith("l0") else "post") in on:
                            pieces[name](s)

                def turn(q):
                    layer, s = divmod(q, 2)
                    if layer == 0:
                        pe.wait_ge(x1_ready, 2 * gru + s + 1)
                        if s == Y:
                            pe.wait_ge(xT_copied, 2 * gru + 1)
                        transposes(b_t, x1[s], True).then_inc(t_done, 1)
                    else:
                        pe.wait_ge(h_ready, STEPS * gru + q - 1)
                        transposes(b_t, hT[s], False).then_inc(t_done, 1)

                def in_parts(bank, w, m, start, stop):
                    (w_hi, w_lo), (m_hi, m_lo) = w, m
                    nc.tensor.matmul(bank[:], w_hi, m_hi, start=start, stop=False)
                    nc.tensor.matmul(bank[:], w_hi, m_lo, start=False, stop=False)
                    return nc.tensor.matmul(bank[:], w_lo, m_hi, start=False, stop=stop)

                def step(q):
                    layer, s = divmod(q, 2)
                    n = STEPS * gru + q
                    if layer == 0:
                        pe.wait_ge(x1_hi_ready, 2 * gru + s + 1)
                        pe.wait_ge(x1_lo_ready, 2 * gru + s + 1)
                        pe.wait_ge(a_hi_ready[s], NT * (gru + 1))
                        pe.wait_ge(a_lo_ready[s], NT * (gru + 1))
                    else:
                        pe.wait_ge(hn_lo_ready, (STEPS - 2) * gru + q - 1)
                    for t in range(NT):
                        last = in_parts(b_u, (hn_hi[s][:, t, :], hn_lo[s][:, t, :]),
                                        (a_hi[s][:, t, :], a_lo[s][:, t, :]), t == 0, t == NT - 1)
                    last.then_inc(u_done, 1)
                    fill(3 * q)
                    if q > 0 or not (isinstance(gru, int) and gru == 0):
                        pe.wait_ge(ztanh_ready, n)
                        pe.wait_ge(pre_n_ready, n)
                    pe.wait_ge(hT_lo_ready, n + 1)

                    def gate(bank, k, weights, moving, start, stop):
                        w = tuple(part[:, layer, k * C:(k + 1) * C] for part in weights)
                        return in_parts(bank, w, moving, start, stop)

                    h_parts = (hT_hi[s][:], hT_lo[s][:])
                    u_parts = (uT_hi[s][:], uT_lo[s][:])
                    gate(b_hn, 2, (wh_hi, wh_lo), h_parts, True, True).then_inc(ghn_done, 1)
                    gate(b_r, 0, (wh_hi, wh_lo), h_parts, True, False)
                    gate(b_z, 1, (wh_hi, wh_lo), h_parts, True, False)
                    pe.wait_ge(u_lo_ready, n + 1)
                    gate(b_r, 0, (wg_hi, wg_lo), u_parts, False, True).then_inc(gr_done, 1)
                    gate(b_xn, 2, (wg_hi, wg_lo), u_parts, True, True).then_inc(gxn_done, 1)
                    if q + 1 < STEPS:
                        turn(q + 1)
                    gate(b_z, 1, (wg_hi, wg_lo), u_parts, False, True).then_inc(gz_done, 1)
                    fill(3 * q + 1)

                if "post" in on:
                    post_back(X)
                if "gru" in on:
                    turn(0)
                for q in range(STEPS):
                    if "gru" in on:
                        step(q)
                    else:
                        if "setup" in on and q == SETUP_STEP:
                            setup()
                        for point in range(3 * q, 3 * q + 3):
                            fill(point)

            bodies(pe, body)

        @block.scalar
        def _(act):
            def setup():
                act.wait_ge(weights_in, 16 * 11)
                nc.scalar.activation(wh_hi[:], whht, ACT.Copy).then_inc(setup_act, 1)
                for layer, b in enumerate((b_r, b_z, b_xn, b_hn)):
                    act.wait_ge(setup_pe, layer + 1)
                    nc.scalar.activation(wg_hi[:, layer, :], b[:, 0:G], ACT.Copy).then_inc(setup_act, 1)
                act.wait_ge(setup_pe, L + 2)
                nc.scalar.activation(arow[:, :, :].rearrange("p e c -> p (e c)"), b_u[:, 0:2 * C], ACT.Copy)\
                    .then_inc(setup_copied, 1)
                act.wait_ge(setup_dve, 2)

            def body(pre, gru, post, on):
                def degree(s):
                    act.wait_ge(araw_in[s], 16 * (pre + 1))
                    if s == Y or not (isinstance(pre, int) and pre == 0):
                        act.wait_ge(dd_ready, 2 * pre + s)
                    for t in range(NT):
                        last = nc.scalar.activation(scratch[:, t, :], a_raw[s][:, t, :], ACT.Copy,
                                                    accum_out=deg[:, t:t + 1])
                    last.then_inc(deg_ready, 1)

                def split_a(s):
                    if "gru" in on:
                        act.wait_ge(u_done, STEPS * gru + STEPS - 1 + s)
                    for t in range(NT):
                        nc.scalar.activation(a_hi[s][:, t, :], a_raw[s][:, t, :], ACT.Copy)\
                            .then_inc(a_hi_ready[s], 1)

                def split_x1(s):
                    if "gru" in on:
                        act.wait_ge(u_done, STEPS * gru + STEPS - 1 + s)
                    act.wait_ge(x1_ready, 2 * pre + s + 1)
                    nc.scalar.activation(hn_hi[s][:], x1[s][:], ACT.Copy).then_inc(x1_hi_ready, 1)

                def agg_copy(kind, s, run, dst):
                    act.wait_ge(agg_done[kind], 2 * run + s + 1)
                    nc.scalar.activation(dst[:], b_agg[:], ACT.Copy).then_inc(agg_copied[kind], 1)

                def agg_l0(s):
                    agg_copy("l0", s, pre, agg_pre)

                def agg_att(s):
                    agg_copy("att", s, post, agg[s])

                def agg_l3(s):
                    agg_copy("l3", s, post, agg[s])

                def att_bcast(s):
                    act.wait_ge(lin_done["bcast"], 2 * post + s + 1)
                    nc.scalar.activation(es[s][:], b_lin[:], ACT.Copy).then_inc(lin_read["bcast"], 1)

                def att_er(s):
                    for t in range(NT):
                        act.wait_ge(umax_ready, NT * (2 * post + s) + t + 1)
                        nc.scalar.activation(att[s][:, t, :], att[s][:, t, :], ACT.Identity,
                                             bias=ecol[s][:, 1, t:t + 1]).then_inc(logit_ready, 1)

                def att_exp(s):
                    g = 2 * post + s
                    act.wait_ge(nmx_ready, g + 1)
                    for t in range(NT):
                        act.wait_ge(lrelu_ready, NT * g + t + 1)
                        nc.scalar.activation(att[s][:, t, :], att[s][:, t, :], ACT.Exp, bias=nmx[s][:, t:t + 1],
                                             accum_out=den[s][:, t:t + 1]).then_inc(exp_ready, 1)

                def store(s):
                    act.wait_ge(out_ready, 2 * post + s + 1)
                    act.dma_start(out[2 * post + s], xs[s][:]).then_inc(out_stored[s], 16)

                pieces = dict(degree=degree, split_a=split_a, split_x1=split_x1, agg_l0=agg_l0, agg_att=agg_att, agg_l3=agg_l3,
                              att_bcast=att_bcast, att_er=att_er, att_exp=att_exp, store=store)

                def fill(point):
                    for name, s in ACT_FILL.get(point, ()):
                        if ("pre" if name in ("degree", "agg_l0", "split_a", "split_x1") else "post") in on:
                            pieces[name](s)

                def step(q):
                    layer, s = divmod(q, 2)
                    n = STEPS * gru + q
                    if q == 0:
                        copy_xT(X)
                        split_h(0)
                    act.wait_ge(u_done, n + 1)
                    nc.scalar.activation(uT_hi[s][:], b_u[:], ACT.Copy).then_inc(u_hi_ready, 1)
                    if 2 <= q + 1 < STEPS:
                        split_h(q + 1)
                    fill(3 * q)
                    act.wait_ge(ghn_done, n + 1)
                    nc.scalar.activation(hb[s][:], b_hn[:], ACT.Identity, bias=half_b[:, layer, 2:3], scale=0.5)
                    act.wait_ge(gr_done, n + 1)
                    nc.scalar.activation(rg[s][:], b_r[:], ACT.Tanh, bias=half_b[:, layer, 0:1], scale=0.5)\
                        .then_inc(r_ready, 1)
                    if q == 0:
                        copy_xT(Y)
                        split_h(1)
                    elif q + 1 < STEPS:
                        act.wait_ge(t_done, n + 2)
                        nc.scalar.activation(hn_hi[1 - s][:], tiles(b_t[:]), ACT.Copy).then_inc(hn_hi_ready, 1)
                    act.wait_ge(gz_done, n + 1)
                    nc.scalar.activation(zg[s][:], b_z[:], ACT.Tanh, bias=half_b[:, layer, 1:2], scale=0.5)\
                        .then_inc(ztanh_ready, 1)
                    act.wait_ge(ztanh_ready, n + 1)
                    nc.scalar.activation(zg[s][:], zg[s][:], ACT.Copy, bias=0.5, scale=0.5)\
                        .then_inc(z_ready, 1)
                    fill(3 * q + 1)
                    act.wait_ge(pre_n_ready, n + 1)
                    nc.scalar.activation(ng[s][:], hb[s][:], ACT.Tanh, bias=bih[:, layer, 2:3])\
                        .then_inc(n_ready, 1)
                    fill(3 * q + 2)

                def copy_xT(s):
                    if "post" in on:
                        act.wait_ge(back_done, 2 * post + s + 1)
                    act.wait_ge(t_done, STEPS * gru + s + 1)
                    nc.scalar.activation(hT[s][:], b_t[:], ACT.Copy).then_inc(xT_copied, 1)
                    act.wait_ge(xT_copied, 2 * gru + s + 1)

                def split_h(q):
                    s = q % 2
                    if q >= 2:
                        act.wait_ge(h_ready, STEPS * gru + q - 1)
                    nc.scalar.activation(hT_hi[s][:], hT[s][:], ACT.Copy).then_inc(hT_hi_ready, 1)

                for q in range(STEPS):
                    if "gru" in on:
                        step(q)
                    else:
                        if "setup" in on and q == SETUP_STEP:
                            setup()
                        for point in range(3 * q, 3 * q + 3):
                            fill(point)

            bodies(act, body)

        @block.vector
        def _(dve):
            def setup():
                dve.wait_ge(weights_in, 16 * 11)
                dve.wait_ge(setup_pool, 2)
                dve.wait_ge(setup_act, 1)
                nc.vector.tensor_tensor(wh_lo[:], whht, wh_hi[:].bitcast(F32), ALU.subtract)
                for e in range(2):
                    last = nc.vector.tensor_scalar(acols[:, e, :], ones[:], avec[:, e:e + 1], None, ALU.mult)
                last.then_inc(setup_dve, 1)
                nc.vector.tensor_tensor(half_b[:, :, 0:2], bih[:, :, 0:2], bhh[:, :, 0:2], ALU.add)
                nc.vector.tensor_copy(half_b[:, :, 2:3], bhh[:, :, 2:3]).then_inc(setup_copied, 1)
                for layer, b in enumerate((b_r, b_z, b_xn, b_hn)):
                    dve.wait_ge(setup_act, layer + 2)
                    nc.vector.tensor_tensor(wg_lo[:, layer, :], b[:, 0:G], wg_hi[:, layer, :].bitcast(F32),
                                            ALU.subtract).then_inc(setup_copied, 1)
                dve.wait_ge(setup_copied, L + 2)
                nc.vector.tensor_scalar(half_b[:], half_b[:], 0.5, None, ALU.mult).then_inc(setup_dve, 1)

            def body(pre, gru, post, on):
                marks = {"pre": 0, "post": 0}
                runs = {"pre": pre, "post": post}

                def link(flow, ins):
                    marks[flow] += 1
                    ins.then_inc(chain_sem[flow], 1)
                    dve.wait_ge(chain_sem[flow], DVE_LINKS[flow] * runs[flow] + marks[flow])

                def own():
                    dve.wait_ge(setup_dve, 2)

                def statistics(kind, s, src):
                    flow = flow_of[kind]
                    k = (flow, s)
                    for t in range(NT):
                        last = nc.vector.bn_stats(stats[:, t, :], src[:, t, :])
                    link(flow, last)
                    even, odd = stats[:, :, 1:3], stats[:, :, 4:6]
                    nc.vector.tensor_tensor(both[k][:], even, odd, ALU.add)
                    link(flow, nc.vector.tensor_tensor(dif[k][:], even[:, :, 0], odd[:, :, 0], ALU.subtract))
                    nc.vector.tensor_scalar(mean[k][:], both[k][:, :, 0], 0.5, None, ALU.mult)
                    nc.vector.tensor_scalar(ve[k][:], both[k][:, :, 1], 1.0 / C, LN_EPS, ALU.mult, ALU.add)
                    link(flow, nc.vector.scalar_tensor_tensor(dif[k][:], dif[k][:], 0.25, dif[k][:],
                                                              ALU.mult, ALU.mult))
                    nc.vector.tensor_tensor(ve[k][:], ve[k][:], dif[k][:], ALU.add)\
                        .then_inc(var_ready[kind], 1)

                def normalise(kind, s, src, dst, ready):
                    k = (flow_of[kind], s)
                    dve.wait_ge(rstd_ready[kind], 2 * runs[flow_of[kind]] + s + 1)
                    for t in range(NT):
                        last = nc.vector.tensor_scalar(dst[:, t, :], src[:, t, :], mean[k][:, t:t + 1],
                                                       rstd[k][:, t:t + 1], ALU.subtract, ALU.mult)
                    if ready is None:
                        link(flow_of[kind], last)
                    else:
                        last.then_inc(ready, 1)

                def post_read(s):
                    g = 2 * post + s
                    dve.wait_ge(back_done, g + 1)
                    m = nmask[:, bass.ds(g, 1), :].rearrange("p b t -> p (b t)")
                    nc.vector.tensor_tensor(x2[s][:], tiles(back_bank[s][:]), bc(m), ALU.mult).then_inc(back_read, 1)

                def post_res(s):
                    dve.wait_ge(back_read, 2 * post + s + 1)
                    link("post", nc.vector.tensor_tensor(x2[s][:], x2[s][:], res[s][:], ALU.add))
                    keep_x1(s)
                    statistics("post", s, x2[s])

                def keep_x1(s):
                    if "gru" in on:
                        dve.wait_ge(x1_ready, 2 * gru + s + 1)
                        nc.vector.tensor_copy(res[s][:], x1[s][:]).then_inc(res_kept, 1)

                def norm_post(s):
                    normalise("post", s, x2[s], x2[s], None)

                def mask(s):
                    dve.wait_ge(at_in[s], 16 * (post + 1))
                    nc.vector.tensor_scalar(att[s][:], at[s][:], 0.0, MASKED, ALU.is_le, ALU.mult)\
                        .then_inc(mask_ready, 1)

                def att_scores(s):
                    if not (isinstance(post, int) and post == 0):
                        own()
                        dve.wait_ge(out_stored[s], 16 * post)
                    for e in range(2):
                        for t in range(NT):
                            last = nc.vector.tensor_tensor_reduce(
                                out=(tiles(agg[s][:]), xs[s])[e][:, t, :], in0=x2[s][:, t, :], in1=arow[:, e, :], scale=1.0, scalar=0.0,
                                op0=ALU.mult, op1=ALU.add, accum_out=ecol[s][:, e, t:t + 1])
                    link("post", last)
                    nc.vector.tensor_tensor(tiles(es[s][:]), ident[:].unsqueeze(1).to_broadcast([P, NT, P]),
                                            bc(ecol[s][:, 0, :]), ALU.mult).then_inc(ediag_ready, 1)

                def att_max(s):
                    g = 2 * post + s
                    own()
                    dve.wait_ge(lin_read["bcast"], g + 1)
                    dve.wait_ge(maskdiag_ready, g + 1)
                    for t in range(NT):
                        last = nc.vector.tensor_tensor_reduce(
                            out=att[s][:, t, :], in0=att[s][:, t, :], in1=es[s][:], scale=1.0, scalar=-3e38,
                            op0=ALU.add, op1=ALU.max, accum_out=mx[s][:, t:t + 1])
                        last.then_inc(umax_ready, 1)
                    dve.wait_ge(umax_ready, NT * g + NT)
                    link("post", nc.vector.tensor_tensor(mx[s][:], mx[s][:], ecol[s][:, 1, :], ALU.add))
                    link("post", nc.vector.scalar_tensor_tensor(mx[s][:], mx[s][:], SLOPE, mx[s][:],
                                                                ALU.mult, ALU.max))
                    nc.vector.tensor_scalar(nmx[s][:], mx[s][:], -1.0, None, ALU.mult).then_inc(nmx_ready, 1)

                def att_lrelu(s):
                    g = 2 * post + s
                    for t in range(NT):
                        dve.wait_ge(logit_ready, NT * g + t + 1)
                        nc.vector.scalar_tensor_tensor(att[s][:, t, :], att[s][:, t, :], SLOPE, att[s][:, t, :],
                                                       ALU.mult, ALU.max).then_inc(lrelu_ready, 1)

                def att_weight(s):
                    dve.wait_ge(exp_ready, NT * (2 * post + s + 1))
                    link("post", nc.vector.reciprocal(rden[s][:], den[s][:]))
                    nc.vector.tensor_tensor(xs[s][:], x2[s][:], bc(rden[s][:]), ALU.mult).then_inc(xs2_ready, 1)

                def att_res(s):
                    dve.wait_ge(lin_done["att"], 2 * post + s + 1)
                    nc.vector.tensor_tensor(x3[s][:], tiles(b_lin[:]), x2[s][:], ALU.add)\
                        .then_inc(lin_read["att"], 1)
                    dve.wait_ge(lin_read["att"], 2 * post + s + 1)
                    statistics("att", s, x3[s])

                def norm_att(s):
                    normalise("att", s, x3[s], x3[s], x3_ready)
                    dve.wait_ge(x3_ready, 2 * post + s + 1)
                    nc.vector.tensor_tensor(xs[s][:], x3[s][:], bc(d3_post[:, s, :]), ALU.mult)\
                        .then_inc(xs3_ready, 1)

                def l3_res(s):
                    g = 2 * post + s
                    dve.wait_ge(lin_done["l3"], g + 1)
                    nc.vector.tensor_tensor(x2[s][:], tiles(b_lin[:]), bc(d3_post[:, s, :]), ALU.mult)\
                        .then_inc(lin_read["l3"], 1)
                    dve.wait_ge(lin_read["l3"], g + 1)
                    dve.wait_ge(xb_ready, g + 1)
                    link("post", nc.vector.tensor_tensor(x2[s][:], x2[s][:], x3[s][:], ALU.add))
                    statistics("l3", s, x2[s])

                def norm_l3(s):
                    normalise("l3", s, x2[s], xs[s], out_ready)

                def l0_degree(s):
                    g = 2 * pre + s
                    dve.wait_ge(adiag_ready, g + 1)
                    link("pre", nc.vector.reduce_sum(ann[:], adiag[:], AX_X))
                    dve.wait_ge(deg_ready, g + 1)
                    link("pre", nc.vector.tensor_tensor(ann[:], deg[:], ann[:], ALU.subtract))
                    nc.vector.tensor_scalar(dd[:, 0:NT], ann[:], 1.0, None, ALU.add)
                    nc.vector.tensor_scalar(dd[:, NT:2 * NT], deg[:], DEG_EPS, None, ALU.add)\
                        .then_inc(dd_ready, 1)

                def l0_scale(s):
                    g = 2 * pre + s
                    dve.wait_ge(ddp_ready, g + 1)
                    link("pre", nc.vector.tensor_scalar(d0[:], ddp[:, 0:NT], DEG_EPS, None, ALU.add))
                    link("pre", nc.vector.reciprocal(d0[:], d0[:]))
                    nc.vector.tensor_copy(d3_pre[:, s, :], ddp[:, NT:2 * NT])
                    dve.wait_ge(x0_in[s], 16 * (pre + 1))
                    if s == Y or not (isinstance(pre, int) and pre == 0):
                        dve.wait_ge(agg_done["l0"], g)
                    nc.vector.tensor_tensor(xs_pre[:], x0[s][:], bc(d0[:]), ALU.mult).then_inc(xs0_ready, 1)

                def l0_res(s):
                    g = 2 * pre + s
                    dve.wait_ge(lin_done["l0"], g + 1)
                    nc.vector.tensor_tensor(y_pre[:], tiles(b_lin[:]), bc(d0[:]), ALU.mult)\
                        .then_inc(lin_read["l0"], 1)
                    dve.wait_ge(lin_read["l0"], g + 1)
                    nc.vector.scalar_tensor_tensor(y_pre[:], y_pre[:], 0.0, x0[s][:], ALU.max, ALU.add)\
                        .then_inc(x0_used, 1)
                    dve.wait_ge(x0_used, g + 1)
                    statistics("l0", s, y_pre)

                def split_x1(s):
                    dve.wait_ge(x1_hi_ready, 2 * pre + s + 1)
                    nc.vector.tensor_tensor(hn_lo[s][:], x1[s][:], hn_hi[s][:].bitcast(F32), ALU.subtract)\
                        .then_inc(x1_lo_ready, 1)

                def norm_l0(s):
                    if "gru" in on:
                        dve.wait_ge(t_done, STEPS * gru + s + 1)
                        dve.wait_ge(res_kept, 2 * gru + s + 1)
                    normalise("l0", s, y_pre, x1[s], x1_ready)

                pieces = dict(post_read=post_read, post_res=post_res, norm_post=norm_post, mask=mask, att_scores=att_scores,
                              att_max=att_max, att_lrelu=att_lrelu, att_weight=att_weight, att_res=att_res,
                              norm_att=norm_att, l3_res=l3_res, norm_l3=norm_l3, l0_degree=l0_degree,
                              l0_scale=l0_scale, l0_res=l0_res, norm_l0=norm_l0, split_x1=split_x1)
                of_pre = ("l0_degree", "l0_scale", "l0_res", "norm_l0", "split_x1")

                def fill(point):
                    for name, s in DVE_FILL.get(point, ()):
                        if ("pre" if name in of_pre else "post") in on:
                            pieces[name](s)
                        elif name == "post_res" and "gru" in on:
                            keep_x1(s)

                def step(q):
                    s = q % 2
                    n = STEPS * gru + q
                    dve.wait_ge(u_hi_ready, n + 1)
                    nc.vector.tensor_tensor(uT_lo[s][:], b_u[:], uT_hi[s][:].bitcast(F32), ALU.subtract)\
                        .then_inc(u_lo_ready, 1)
                    fill(3 * q)
                    dve.wait_ge(r_ready, n + 1)
                    nc.vector.scalar_tensor_tensor(hb[s][:], rg[s][:], 1.0, hb[s][:], ALU.add, ALU.mult)\
                        .then_inc(t_ready, 1)
                    dve.wait_ge(gxn_done, n + 1)
                    dve.wait_ge(t_ready, n + 1)
                    nc.vector.tensor_tensor(hb[s][:], b_xn[:], hb[s][:], ALU.add).then_inc(pre_n_ready, 1)
                    if 2 <= q + 1 < STEPS:
                        dve.wait_ge(hn_hi_ready, (STEPS - 2) * gru + q)
                        nc.vector.tensor_tensor(hn_lo[1 - s][:], tiles(b_t[:]), hn_hi[1 - s][:].bitcast(F32),
                                                ALU.subtract).then_inc(hn_lo_ready, 1)
                    fill(3 * q + 1)
                    dve.wait_ge(n_ready, n + 1)
                    nc.vector.scalar_tensor_tensor(ng[s][:], zg[s][:], 1.0, ng[s][:], ALU.subtract, ALU.mult)\
                        .then_inc(w_ready, 1)
                    dve.wait_ge(w_ready, n + 1)
                    dve.wait_ge(zh_ready, n + 1)
                    nc.vector.tensor_tensor(hT[s][:], zh[s][:], ng[s][:], ALU.subtract).then_inc(h_ready, 1)
                    fill(3 * q + 2)

                if "post" in on:
                    link("post", nc.vector.tensor_copy(d3_post[:], d3_gru[:]))
                if "gru" in on:
                    nc.vector.tensor_copy(d3_gru[:], d3_pre[:])
                fill(-1)
                for q in range(STEPS):
                    if "gru" in on:
                        step(q)
                    else:
                        if "setup" in on and q == SETUP_STEP:
                            setup()
                        for point in range(3 * q, 3 * q + 3):
                            fill(point)
                for flow in ("pre", "post"):
                    assert flow not in on or marks[flow] == DVE_LINKS[flow], (flow, marks[flow])

            bodies(dve, body)

        @block.gpsimd
        def _(pool):
            nc.gpsimd.memset(ones[:], 1.0).then_inc(setup_pool, 1)
            pool.wait_ge(setup_pool, 1)
            nc.gpsimd.affine_select(out=ident[:], in_=ones[:], compare_op=ALU.is_equal, fill=0.0, base=0,
                                    pattern=[[-1, P]], channel_multiplier=1).then_inc(setup_pool, 1)
            nc.gpsimd.memset(exps[:, 0:NT], 0.5).then_inc(setup_pool, 1)
            nc.gpsimd.memset(exps[:, NT:2 * NT], -0.5).then_inc(setup_pool, 1)
            pool.wait_ge(setup_pool, 4)

            def setup():
                pool.wait_ge(weights_in, 16 * 11)

            def body(pre, gru, post, on):
                runs = {"pre": pre, "post": post}

                def one_diagonal(m, value, ready):
                    d = diagonal(m)
                    nc.gpsimd.affine_select(out=d, in_=d, compare_op=ALU.not_equal, fill=value, base=0,
                                            pattern=[[0, NT], [-1, P]], channel_multiplier=1).then_inc(ready, 1)

                def wait_apart(sem, count):
                    count = count if isinstance(count, int) else pool.to_reg(count)
                    pool.wait_ge(setup_pool, 4)
                    pool.wait_ge(sem, count)

                def diag_a(s):
                    pool.wait_ge(araw_in[s], 16 * (pre + 1))
                    if s == Y or not (isinstance(pre, int) and pre == 0):
                        pool.wait_ge(dd_ready, 2 * pre + s)
                    nc.gpsimd.tensor_tensor(adiag[:], diagonal(a_raw[s]), ident[:].unsqueeze(1)
                                            .to_broadcast([P, NT, P]), ALU.mult).then_inc(adiag_ready, 1)

                def diag_at(s):
                    wait_apart(atpre_in, 16 * (2 * pre + s + 1))
                    one_diagonal(at_pre, 1.0, atdiag_ready)

                def split_a(s):
                    for t in range(NT):
                        pool.wait_ge(a_hi_ready[s], NT * pre + t + 1)
                        nc.gpsimd.tensor_tensor(a_lo[s][:, t, :], a_raw[s][:, t, :], a_hi[s][:, t, :].bitcast(F32),
                                                ALU.subtract).then_inc(a_lo_ready[s], 1)

                def powers(s):
                    pool.wait_ge(dd_ready, 2 * pre + s + 1)
                    nc.gpsimd.tensor_tensor(ddp[:], dd[:], exps[:], ALU.pow).then_inc(ddp_ready, 1)

                def mask_diag(s):
                    wait_apart(mask_ready, 2 * post + s + 1)
                    one_diagonal(att[s], 0.0, maskdiag_ready)

                def add_bias(s):
                    pool.wait_ge(xs3_ready, 2 * post + s + 1)
                    nc.gpsimd.tensor_tensor(x3[s][:], x3[s][:], bias3[:].unsqueeze(1)
                                            .to_broadcast([P, NT, C]), ALU.add).then_inc(xb_ready, 1)

                def rstd_of(kind):
                    flow = flow_of[kind]

                    def piece(s):
                        pool.wait_ge(var_ready[kind], 2 * runs[flow] + s + 1)
                        nc.gpsimd.tensor_tensor(rstd[flow, s][:], ve[flow, s][:], exps[:, NT:2 * NT], ALU.pow)\
                            .then_inc(rstd_ready[kind], 1)
                    return piece

                pieces = dict(split_a=split_a, diag_a=diag_a, diag_at=diag_at, powers=powers, mask_diag=mask_diag,
                              add_bias=add_bias, **{f"rstd_{k}": rstd_of(k) for k in ("post", "att", "l3", "l0")})
                of_pre = ("diag_a", "diag_at", "powers", "rstd_l0", "split_a")

                def fill(point):
                    for name, s in POOL_FILL.get(point, ()):
                        if ("pre" if name in of_pre else "post") in on:
                            pieces[name](s)

                def split_h(q):
                    pool.wait_ge(hT_hi_ready, STEPS * gru + q + 1)
                    nc.gpsimd.tensor_tensor(hT_lo[q % 2][:], hT[q % 2][:], hT_hi[q % 2][:].bitcast(F32),
                                            ALU.subtract).then_inc(hT_lo_ready, 1)

                for q in range(STEPS):
                    if "gru" in on:
                        n, s = STEPS * gru + q, q % 2
                        if q == 0:
                            split_h(0)
                            split_h(1)
                        elif q + 1 < STEPS:
                            split_h(q + 1)
                        fill(3 * q)
                        pool.wait_ge(z_ready, n + 1)
                        nc.gpsimd.tensor_tensor(zh[s][:], zg[s][:], hT[s][:], ALU.mult).then_inc(zh_ready, 1)
                    else:
                        if "setup" in on and q == SETUP_STEP:
                            setup()
                        fill(3 * q)
                    fill(3 * q + 1)
                    fill(3 * q + 2)

            bodies(pool, body)


def kernel(x, adj, nodemask, L0_gnn_kernel, L1_gnn_weight, L1_gnn_w_ih, L1_gnn_w_hh, L1_gnn_b_ih, L1_gnn_b_hh,
           L2_gnn_W_pre, L2_gnn_a_snd, L2_gnn_a_rec, L3_gnn_weight, L3_gnn_bias):
    import numpy as np
    import concourse.bacc as bacc
    from concourse import mybir as mb
    from concourse.bass_utils import run_bass_kernel_spmd as run

    x, adj = np.asarray(x), np.asarray(adj)
    B, N, C = x.shape
    P = 128
    NT = N // P

    def tiled(m):
        return m.reshape(B, NT, P, m.shape[-1]).transpose(0, 2, 1, 3)

    L = np.asarray(L1_gnn_weight).shape[0]
    arrays = {
        "x": tiled(x),
        "adj": tiled(adj),
        "adjt": tiled(adj.transpose(0, 2, 1)),
        "nodemask": np.asarray(nodemask).reshape(B, NT, P).transpose(2, 0, 1),
        "k0": np.asarray(L0_gnn_kernel),
        "w1t": np.asarray(L1_gnn_weight).transpose(2, 0, 1),
        "wiht": np.asarray(L1_gnn_w_ih).transpose(2, 0, 1),
        "whht": np.asarray(L1_gnn_w_hh).transpose(2, 0, 1),
        "bih": np.asarray(L1_gnn_b_ih).reshape(L, 3, C).transpose(2, 0, 1),
        "bhh": np.asarray(L1_gnn_b_hh).reshape(L, 3, C).transpose(2, 0, 1),
        "wpre": np.asarray(L2_gnn_W_pre),
        "wpret": np.asarray(L2_gnn_W_pre).T,
        "avec": np.stack([np.asarray(L2_gnn_a_snd), np.asarray(L2_gnn_a_rec)], axis=1),
        "w3": np.asarray(L3_gnn_weight),
        "bias3": np.asarray(L3_gnn_bias).reshape(1, C),
    }
    arrays = {f"in_{k}": np.ascontiguousarray(v) for k, v in arrays.items()}
    nc = bacc.Bacc("TRN2", target_bir_lowering=False, num_devices=1)
    ins = [nc.dram_tensor(k, v.shape, mb.dt.from_np(v.dtype), kind="ExternalInput").ap() for k, v in arrays.items()]
    out = nc.dram_tensor("out", (B, P, NT, C), mb.dt.float32, kind="ExternalOutput").ap()
    gnn_kernel(nc, *ins, out)
    got = run(nc, [arrays], core_ids=[0]).results[0]["out"]
    return np.ascontiguousarray(got.transpose(0, 2, 1, 3).reshape(B, N, C))
```

```python
from contextlib import ExitStack

import concourse.bass as bass
from concourse import mybir

ALU = mybir.AluOpType
ACT = mybir.ActivationFunctionType
F32 = mybir.dt.float32
F32R = mybir.dt.float32r
BF16 = mybir.dt.bfloat16
AX_X = mybir.AxisListType.X

P = 128
MASKED = -1e30
LN_EPS = 1e-5
DEG_EPS = 1e-6
SLOPE = 0.2

SETUP_STEP = 7

X, Y = 0, 1

PE_FILL = {
    0: [("post_back", Y)],
    4: [("att_bcast", X)],
    7: [("att_bcast", Y)],
    9: [("att_agg", X)],
    10: [("l0_agg", X), ("att_lin", X)],
    13: [("l3_agg", X), ("l0_lin", X)],
    15: [("l3_lin", X), ("att_agg", Y)],
    16: [("l0_agg", Y), ("att_lin", Y)],
    18: [("l0_lin", Y)],
    19: [("l3_agg", Y)],
    21: [("l3_lin", Y)],
    22: [("turn", X), ("post_back", X)],
}
ACT_FILL = {
    0: [("split_a_0", Y), ("split_a_1", Y), ("split_x1", Y)],
    1: [("degree", X)],
    2: [("norm_post", X)],
    4: [("att_bcast", X)],
    5: [("degree", Y), ("norm_post", Y)],
    6: [("att_er_0", X)],
    7: [("att_er_1", X)],
    8: [("att_exp_0", X), ("att_exp_1", X), ("att_bcast", Y)],
    9: [("att_er_0", Y), ("att_er_1", Y), ("agg_att", X)],
    10: [("agg_l0", X)],
    11: [("att_exp_0", Y), ("att_exp_1", Y)],
    12: [("norm_att", X)],
    14: [("agg_l3", X), ("norm_l0", X)],
    15: [("agg_att", Y)],
    17: [("agg_l0", Y), ("split_x1", X)],
    18: [("norm_att", Y)],
    19: [("norm_l3", X)],
    20: [("split_a_0", X), ("agg_l3", Y)],
    21: [("split_a_1", X)],
    22: [("norm_l0", Y)],
    23: [("norm_l3", Y), ("copy_xT", X)],
}
DVE_FILL = {
    -1: [("post_res", X), ("post_read", Y), ("stats_post", X)],
    0: [("keep_x1", X), ("mask", X), ("split_x1", Y)],
    1: [("post_res", Y), ("stats_post", Y), ("l0_degree", X)],
    3: [("att_scores", X)],
    4: [("mask", Y)],
    5: [("att_max_0", X), ("att_max_1", X)],
    6: [("att_scores", Y)],
    7: [("att_lrelu_0", X), ("att_lrelu_1", X), ("att_weight", X)],
    8: [("l0_scale", X), ("keep_x1", Y)],
    9: [("att_max_0", Y), ("att_max_1", Y), ("att_lrelu_0", Y), ("l0_degree", Y)],
    10: [("att_lrelu_1", Y), ("att_res", X), ("stats_att", X)],
    12: [("att_weight", Y), ("att_scale", X)],
    13: [("l0_res", X), ("stats_l0", X)],
    14: [("l0_scale", Y)],
    15: [("l3_res", X), ("stats_l3", X)],
    16: [("att_res", Y), ("stats_att", Y)],
    18: [("att_scale", Y)],
    19: [("l0_res", Y)],
    20: [("stats_l0", Y)],
    21: [("l3_res", Y), ("stats_l3", Y)],
    22: [("split_x1", X)],
    23: [("post_read", X)],
}
POOL_FILL = {
    0: [("diag_a", X), ("split_a_0", Y), ("split_a_1", Y), ("rstd_post", X)],
    1: [("rstd_post", Y)],
    3: [("mask_diag", X)],
    4: [("powers", X), ("diag_at", X)],
    8: [("mask_diag", Y), ("diag_a", Y)],
    10: [("rstd_att", X)],
    12: [("powers", Y)],
    13: [("rstd_l0", X)],
    15: [("add_bias", X), ("diag_at", Y)],
    16: [("rstd_att", Y), ("rstd_l3", X)],
    17: [("add_bias", Y)],
    19: [("split_a_0", X), ("rstd_l0", Y), ("split_a_1", X)],
    21: [("rstd_l3", Y)],
    22: [("split_xT", X)],
}


def gnn_kernel(nc, x_in, adj_in, adjt_in, mask_in, k0_in, w1t_in, wiht_in, whht_in, bih_in, bhh_in,
               wpre_in, wpret_in, avec_in, w3_in, bias3_in, out):
    B, _, NT, C = x_in.shape
    N = NT * P
    L = w1t_in.shape[1]
    PAIRS = B // 2
    G = 3 * C
    STEPS = 2 * L
    DVE_LINKS = {"pre": 14, "post": 31}

    with ExitStack() as ctx:
        def sb(name, shape, dtype=F32):
            return ctx.enter_context(nc.sbuf_tensor(name, shape, dtype))

        def bank(name):
            return ctx.enter_context(nc.psum_tensor(name, [P, N], F32))

        def sem(name):
            return ctx.enter_context(nc.semaphore(name))

        ident = sb("ident", [P, P])
        ones = sb("ones", [P, P])
        wg_hi = sb("wg_hi", [P, L, G], F32R)
        wg_lo = sb("wg_lo", [P, L, G], F32R)
        wh_hi = sb("wh_hi", [P, L, G], F32R)
        wh_lo = sb("wh_lo", [P, L, G], F32R)
        bih = sb("bih", [P, L, 3])
        bhh = sb("bhh", [P, L, 3])
        half_b = sb("half_b", [P, L, 3])
        k0 = sb("k0", [P, C])
        wpre = sb("wpre", [P, C])
        w3 = sb("w3", [P, C])
        avec = sb("avec", [P, 2])
        arow = sb("arow", [P, 2, C])
        bias3 = sb("bias3", [P, C])
        nmask = sb("nmask", [P, B, NT])
        exps = sb("exps", [P, 2 * NT])

        a_raw = [sb(f"a_raw_{s}", [P, NT, N]) for s in (X, Y)]
        at_pre = sb("at_pre", [P, NT, N])
        scratch = sb("scratch", [P, NT, N], BF16)
        x0 = [sb(f"x0_{s}", [P, NT, C]) for s in (X, Y)]
        xs_pre = sb("xs_pre", [P, NT, C])
        adiag = sb("adiag", [P, NT, P])
        y_pre = xs_pre
        agg_pre = sb("agg_pre", [P, N])
        x1 = [sb(f"x1_{s}", [P, NT, C]) for s in (X, Y)]
        deg = sb("deg", [P, NT])
        ann = sb("ann", [P, NT])
        dd = sb("dd", [P, 2 * NT])
        ddp = sb("ddp", [P, 2 * NT])
        d0 = sb("d0", [P, NT])
        d3_pre = sb("d3_pre", [P, 2, NT])
        d3_gru = sb("d3_gru", [P, 2, NT])
        d3_post = sb("d3_post", [P, 2, NT])

        a_hi = [sb(f"a_hi_{s}", [P, NT, N], F32R) for s in (X, Y)]
        a_lo = [sb(f"a_lo_{s}", [P, NT, N], F32R) for s in (X, Y)]
        hT = [sb(f"hT_{s}", [P, N]) for s in (X, Y)]
        hT_hi = [sb(f"hT_hi_{s}", [P, N], F32R) for s in (X, Y)]
        hT_lo = [sb(f"hT_lo_{s}", [P, N], F32R) for s in (X, Y)]
        hn_hi = [sb(f"hn_hi_{s}", [P, NT, C], F32R) for s in (X, Y)]
        hn_lo = [sb(f"hn_lo_{s}", [P, NT, C], F32R) for s in (X, Y)]
        uT_hi = [sb(f"uT_hi_{s}", [P, N], F32R) for s in (X, Y)]
        uT_lo = [sb(f"uT_lo_{s}", [P, N], F32R) for s in (X, Y)]
        rg = [sb(f"rg_{s}", [P, N]) for s in (X, Y)]
        zg = [sb(f"zg_{s}", [P, N]) for s in (X, Y)]
        hb = [sb(f"hb_{s}", [P, N]) for s in (X, Y)]
        ng = [sb(f"ng_{s}", [P, N]) for s in (X, Y)]
        zh = [sb(f"zh_{s}", [P, N]) for s in (X, Y)]

        at = [sb(f"at_{s}", [P, NT, N]) for s in (X, Y)]
        att = [sb(f"att_{s}", [P, NT, N]) for s in (X, Y)]
        es = [sb(f"es_{s}", [P, N]) for s in (X, Y)]
        res = [sb(f"res_{s}", [P, NT, C]) for s in (X, Y)]
        x2 = [sb(f"x2_{s}", [P, NT, C]) for s in (X, Y)]
        x3 = [sb(f"x3_{s}", [P, NT, C]) for s in (X, Y)]
        xs = [sb(f"xs_{s}", [P, NT, C]) for s in (X, Y)]
        agg = [sb(f"agg_{s}", [P, N]) for s in (X, Y)]
        ecol = [sb(f"ecol_{s}", [P, 2, NT]) for s in (X, Y)]
        mx = [sb(f"mx_{s}", [P, NT]) for s in (X, Y)]
        nmx = [sb(f"nmx_{s}", [P, NT]) for s in (X, Y)]
        den = [sb(f"den_{s}", [P, NT]) for s in (X, Y)]
        rden = [sb(f"rden_{s}", [P, NT]) for s in (X, Y)]

        wiht, whht = att[X][:, :, 0:G], att[Y][:, :, 0:G]
        w1t = es[X][:, :].rearrange("p (l c) -> p l c", l=L)
        wpret = es[Y][:, 0:C]
        acols = es[Y][:, C:3 * C].rearrange("p (e c) -> p e c", e=2)

        norm_key = [("pre", X), ("pre", Y), ("post", X), ("post", Y)]
        stats = sb("stats", [P, NT, 6])
        both = sb("both", [P, NT, 2])
        dif = sb("dif", [P, NT])
        nmean = {k: sb(f"nmean_{k[0]}{k[1]}", [P, NT]) for k in norm_key}
        shift = {k: sb(f"shift_{k[0]}{k[1]}", [P, NT]) for k in norm_key}
        ve = {k: sb(f"ve_{k[0]}{k[1]}", [P, NT]) for k in norm_key}
        rstd = {k: sb(f"rstd_{k[0]}{k[1]}", [P, NT]) for k in norm_key}

        b_r, b_z, b_xn, b_hn = bank("b_r"), bank("b_z"), bank("b_xn"), bank("b_hn")
        b_u, b_t = bank("b_u"), bank("b_t")
        b_agg, b_lin = bank("b_agg"), bank("b_lin")
        back_bank = (b_agg, b_lin)

        weights_in, k0_loaded = sem("weights_in"), sem("k0_loaded")
        setup_pool, setup_dve, setup_pe, setup_act, setup_copied = (
            sem("setup_pool"), sem("setup_dve"), sem("setup_pe"), sem("setup_act"), sem("setup_copied"))
        araw_in = [sem(f"araw_in_{s}") for s in (X, Y)]
        atpre_in = sem("atpre_in")
        x0_in = [sem(f"x0_in_{s}") for s in (X, Y)]
        at_in = [sem(f"at_in_{s}") for s in (X, Y)]
        out_stored = [sem(f"out_stored_{s}") for s in (X, Y)]

        t_done, xT_copied = sem("t_done"), sem("xT_copied")
        hn_hi_ready, hn_lo_ready = sem("hn_hi_ready"), sem("hn_lo_ready")
        hT_hi_ready, hT_lo_ready = sem("hT_hi_ready"), sem("hT_lo_ready")
        a_hi_ready = [sem(f"a_hi_ready_{s}") for s in (X, Y)]
        a_lo_ready = [sem(f"a_lo_ready_{s}") for s in (X, Y)]
        x1_hi_ready, x1_lo_ready = sem("x1_hi_ready"), sem("x1_lo_ready")
        u_done, u_hi_ready, u_lo_ready = sem("u_done"), sem("u_hi_ready"), sem("u_lo_ready")
        ghn_done, gr_done, gxn_done, gz_done = sem("ghn_done"), sem("gr_done"), sem("gxn_done"), sem("gz_done")
        r_ready, ztanh_ready, z_ready, n_ready = (
            sem("r_ready"), sem("ztanh_ready"), sem("z_ready"), sem("n_ready"))
        t_ready, pre_n_ready, w_ready, h_ready = sem("t_ready"), sem("pre_n_ready"), sem("w_ready"), sem("h_ready")
        zh_ready = sem("zh_ready")

        back_done, back_read = sem("back_done"), sem("back_read")
        res_kept = sem("res_kept")
        x1_ready = sem("x1_ready")
        deg_ready, adiag_ready, dd_ready, ddp_ready = (
            sem("deg_ready"), sem("adiag_ready"), sem("dd_ready"), sem("ddp_ready"))
        atdiag_ready, xs0_ready = sem("atdiag_ready"), sem("xs0_ready")
        x0_used = sem("x0_used")
        agg_done = {k: sem(f"agg_done_{k}") for k in ("l0", "att", "l3")}
        agg_copied = {k: sem(f"agg_copied_{k}") for k in ("l0", "att", "l3")}
        lin_done = {k: sem(f"lin_done_{k}") for k in ("l0", "att", "l3", "bcast")}
        lin_read = {k: sem(f"lin_read_{k}") for k in ("l0", "att", "l3", "bcast")}
        var_ready = {k: sem(f"var_ready_{k}") for k in ("post", "att", "l3", "l0")}
        rstd_ready = {k: sem(f"rstd_ready_{k}") for k in ("post", "att", "l3", "l0")}
        shift_ready = {k: sem(f"shift_ready_{k}") for k in ("post", "att", "l3", "l0")}
        ediag_ready = sem("ediag_ready")
        mask_ready, maskdiag_ready = sem("mask_ready"), sem("maskdiag_ready")
        umax_ready, nmx_ready = sem("umax_ready"), sem("nmx_ready")
        logit_ready, lrelu_ready, exp_ready = sem("logit_ready"), sem("lrelu_ready"), sem("exp_ready")
        x2_ready, xs2_ready, x3_ready, xs3_ready, xb_ready = (
            sem("x2_ready"), sem("xs2_ready"), sem("x3_ready"), sem("xs3_ready"), sem("xb_ready"))
        out_ready = sem("out_ready")
        chain_sem = {k: sem(f"dve_chain_{k}") for k in ("pre", "post")}

        block = ctx.enter_context(nc.Block())

        def bodies(eng, body):
            body(0, 0, 0, {"pre", "setup"})
            body(1, 0, 0, {"pre", "gru"})
            body(2, 1, 0, {"pre", "gru", "post"})
            with eng.Fori(2, PAIRS - 1) as i:
                body(i + 1, i, i - 1, {"pre", "gru", "post"})
            body(PAIRS, PAIRS - 1, PAIRS - 2, {"gru", "post"})
            body(PAIRS, PAIRS, PAIRS - 1, {"post"})

        flow_of = {"l0": "pre", "att": "post", "l3": "post", "bcast": "post", "post": "post"}

        def half(h):
            return range(h * NT // 2, (h + 1) * NT // 2)

        def in_halves(**pieces):
            return {f"{name}_{h}": (lambda s, f=f, h=h: f(s, h)) for name, f in pieces.items() for h in (0, 1)}

        def flow_of_piece(name, s, of_pre):
            if name in ("split_a_0", "split_a_1", "split_x1"):
                return ("pre", "gru")[s]
            if name in ("post_back", "post_read"):
                return ("gru", "post")[s]
            if name == "keep_x1":
                return "gru"
            if name in ("turn", "copy_xT", "split_xT"):
                return "pre"
            return "pre" if name in of_pre else "post"

        def tiles(ap):
            return ap.rearrange("p (t c) -> p t c", t=NT)

        def bc(col):
            return col.unsqueeze(2).to_broadcast([P, NT, C])

        def diagonal(m):
            flat = m[:, :, :].rearrange("p t n -> p (t n)")
            return bass.AP(flat.tensor, flat.offset, [list(flat.ap[0]), [N + P, NT], [1, P]])

        @block.sync
        def _(sp):
            def body(pre, gru, post, on):
                def load_pre(s):
                    g = 2 * pre + s
                    if not is_first(pre):
                        sp.wait_ge(weights_in, 16 * 11)
                        sp.wait_ge(a_lo_ready[s], NT * pre)
                    sp.dma_start(a_raw[s][:], adj_in[g]).then_inc(araw_in[s], 16)
                    if not is_first(pre):
                        sp.wait_ge(weights_in, 16 * 11)
                        sp.wait_ge(x0_used, g - 1)
                    sp.dma_start(x0[s][:], x_in[g]).then_inc(x0_in[s], 16)
                    if "setup" in on and s == X:
                        sp.dma_start(k0[:], k0_in).then_inc(k0_loaded, 16)
                    if "setup" in on and s == Y:
                        load_weights()
                    if s == Y or not is_first(pre):
                        sp.wait_ge(agg_done["l0"], g)
                    sp.dma_start(at_pre[:], adjt_in[g]).then_inc(atpre_in, 16)

                def load_weights():
                    for dst, src in ((w1t, w1t_in), (wiht, wiht_in), (whht, whht_in), (wpret, wpret_in),
                                     (avec[:], avec_in), (bih[:], bih_in), (bhh[:], bhh_in),
                                     (wpre[:], wpre_in), (w3[:], w3_in), (nmask[:], mask_in),
                                     (bias3[:], bias3_in.to_broadcast([P, C]))):
                        sp.dma_start(dst, src).then_inc(weights_in, 16)

                def store(run, s):
                    sp.wait_ge(weights_in, 16 * 11)
                    sp.wait_ge(out_ready, 2 * run + s + 1)
                    sp.dma_start(out[2 * run + s], xs[s][:]).then_inc(out_stored[s], 16)

                def load_post(s):
                    if not is_first(post):
                        sp.wait_ge(weights_in, 16 * 11)
                        sp.wait_ge(agg_done["l3"], 2 * post - 1 + s)
                    sp.dma_start(at[s][:], adjt_in[2 * post + s]).then_inc(at_in[s], 16)

                if "post" in on:
                    load_post(X)
                if "pre" in on:
                    load_pre(X)
                if "post" in on and not is_first(post):
                    store(post - 1, Y)
                if "post" in on:
                    load_post(Y)
                if "pre" in on:
                    load_pre(Y)
                if "post" in on:
                    store(post, X)

            def is_first(run):
                return isinstance(run, int) and run == 0

            bodies(sp, body)
            sp.wait_ge(out_ready, B)
            sp.dma_start(out[B - 1], xs[Y][:]).then_inc(out_stored[Y], 16)
            for s in (X, Y):
                sp.wait_ge(out_stored[s], 16 * PAIRS)

        @block.tensor
        def _(pe):
            def setup():
                pe.wait_ge(weights_in, 16 * 11)
                for layer, b in enumerate((b_r, b_z, b_xn, b_hn)):
                    nc.tensor.matmul(b[:, 0:G], w1t[:, layer, :], wiht[:, layer, :],
                                     start=True, stop=True).then_inc(setup_pe, 1)
                pe.wait_ge(setup_dve, 1)
                for e in range(2):
                    nc.tensor.matmul(b_u[:, e * C:(e + 1) * C], acols[:, e, :], wpret,
                                     start=True, stop=True).then_inc(setup_pe, 1)
                pe.wait_ge(setup_copied, L + 2)
                pe.wait_ge(setup_pool, 2)

            def transposes(bank, src, tiled):
                for t in range(NT):
                    part = src[:, t, :] if tiled else src[:, t * P:(t + 1) * P]
                    last = nc.tensor.transpose(bank[:, t * P:(t + 1) * P], part, ident[:])
                return last

            def body(pre, gru, post, on):
                last_agg, last_lin = [], []

                def free(last, read):
                    if last:
                        pe.wait_ge(*last.pop())
                    elif last is last_agg and "post" in on:
                        pe.wait_ge(back_read, 2 * post + 1)
                    else:
                        if not (isinstance(pre, int) and pre == 0):
                            pe.wait_ge(read["l0"], 2 * pre)
                        if not (isinstance(post, int) and post == 0):
                            pe.wait_ge(read["l3"], 2 * post)

                def free_agg():
                    free(last_agg, agg_copied)

                def free_lin():
                    free(last_lin, lin_read)

                def aggregate(kind, s, run, lhs, rhs):
                    free_agg()
                    for t in range(NT):
                        last = nc.tensor.matmul(b_agg[:], lhs[:, t, :], rhs[:, t, :],
                                                start=(t == 0), stop=(t == NT - 1))
                    last.then_inc(agg_done[kind], 1)
                    last_agg.append((agg_copied[kind], 2 * run + s + 1))

                def linear(kind, s, run, aggT, w):
                    free_lin()
                    pe.wait_ge(agg_copied[kind], 2 * run + s + 1)
                    for t in range(NT):
                        last = nc.tensor.matmul(b_lin[:, t * C:(t + 1) * C], aggT[:, t * P:(t + 1) * P], w[:],
                                                start=True, stop=True)
                    last.then_inc(lin_done[kind], 1)
                    last_lin.append((lin_read[kind], 2 * run + s + 1))

                def post_back(s):
                    run = (gru, post)[s]
                    free_agg() if s == X else free_lin()
                    pe.wait_ge(h_ready, STEPS * run + STEPS - 1 + s)
                    transposes(back_bank[s], hT[s], False).then_inc(back_done, 1)
                    if s == Y:
                        last_lin.append((back_read, 2 * post + 2))

                def att_bcast(s):
                    pe.wait_ge(ediag_ready, 2 * post + s + 1)
                    free_lin()
                    nc.tensor.matmul(b_lin[:], ones[:], es[s][:], start=True, stop=True)\
                        .then_inc(lin_done["bcast"], 1)
                    last_lin.append((lin_read["bcast"], 2 * post + s + 1))

                def att_agg(s):
                    pe.wait_ge(xs2_ready, 2 * post + s + 1)
                    aggregate("att", s, post, xs[s], att[s])

                def att_lin(s):
                    linear("att", s, post, agg[s], wpre)

                def l3_agg(s):
                    pe.wait_ge(at_in[s], 16 * (post + 1))
                    pe.wait_ge(xs3_ready, 2 * post + s + 1)
                    aggregate("l3", s, post, xs[s], at[s])

                def l3_lin(s):
                    linear("l3", s, post, agg[s], w3)

                def l0_agg(s):
                    pe.wait_ge(atdiag_ready, 2 * pre + s + 1)
                    pe.wait_ge(xs0_ready, 2 * pre + s + 1)
                    aggregate("l0", s, pre, xs_pre, at_pre)

                def l0_lin(s):
                    if "setup" in on:
                        pe.wait_ge(k0_loaded, 16)
                    linear("l0", s, pre, agg_pre, k0)

                def turn(q):
                    layer, s = divmod(q, 2)
                    if layer == 0:
                        pe.wait_ge(x1_ready, 2 * (pre, gru)[s] + s + 1)
                        if s == Y:
                            pe.wait_ge(xT_copied, 2 * gru + 1)
                        elif "gru" in on:
                            pe.wait_ge(hn_lo_ready, (STEPS - 2) * (gru + 1))
                        transposes(b_t, x1[s], True).then_inc(t_done, 1)
                    else:
                        pe.wait_ge(h_ready, STEPS * gru + q - 1)
                        transposes(b_t, hT[s], False).then_inc(t_done, 1)

                pieces = dict(post_back=post_back, att_bcast=att_bcast, att_agg=att_agg, att_lin=att_lin,
                              l3_agg=l3_agg, l3_lin=l3_lin, l0_agg=l0_agg, l0_lin=l0_lin,
                              turn=turn)

                def fill(point):
                    for name, s in PE_FILL.get(point, ()):
                        if flow_of_piece(name, s, ("l0_agg", "l0_lin")) in on:
                            pieces[name](s)

                def in_parts(bank, w, m, start, stop):
                    (w_hi, w_lo), (m_hi, m_lo) = w, m
                    nc.tensor.matmul(bank[:], w_hi, m_hi, start=start, stop=False)
                    nc.tensor.matmul(bank[:], w_hi, m_lo, start=False, stop=False)
                    return nc.tensor.matmul(bank[:], w_lo, m_hi, start=False, stop=stop)

                def step(q):
                    layer, s = divmod(q, 2)
                    n = STEPS * gru + q
                    if layer == 0:
                        pe.wait_ge(x1_hi_ready, 2 * gru + s + 1)
                        pe.wait_ge(x1_lo_ready, 2 * gru + s + 1)
                        pe.wait_ge(a_hi_ready[s], NT * (gru + 1))
                        pe.wait_ge(a_lo_ready[s], NT * (gru + 1))
                    else:
                        pe.wait_ge(hn_lo_ready, (STEPS - 2) * gru + q - 1)
                    for t in range(NT):
                        last = in_parts(b_u, (hn_hi[s][:, t, :], hn_lo[s][:, t, :]),
                                        (a_hi[s][:, t, :], a_lo[s][:, t, :]), t == 0, t == NT - 1)
                    last.then_inc(u_done, 1)
                    fill(3 * q)
                    if q > 0 or not (isinstance(gru, int) and gru == 0):
                        pe.wait_ge(ztanh_ready, n)
                        pe.wait_ge(pre_n_ready, n)
                    pe.wait_ge(hT_lo_ready, n + 1)

                    def gate(bank, k, weights, moving, start, stop):
                        w = tuple(part[:, layer, k * C:(k + 1) * C] for part in weights)
                        return in_parts(bank, w, moving, start, stop)

                    h_parts = (hT_hi[s][:], hT_lo[s][:])
                    u_parts = (uT_hi[s][:], uT_lo[s][:])
                    gate(b_hn, 2, (wh_hi, wh_lo), h_parts, True, True).then_inc(ghn_done, 1)
                    gate(b_r, 0, (wh_hi, wh_lo), h_parts, True, False)
                    gate(b_z, 1, (wh_hi, wh_lo), h_parts, True, False)
                    pe.wait_ge(u_lo_ready, n + 1)
                    gate(b_r, 0, (wg_hi, wg_lo), u_parts, False, True).then_inc(gr_done, 1)
                    gate(b_xn, 2, (wg_hi, wg_lo), u_parts, True, True).then_inc(gxn_done, 1)
                    if q + 1 < STEPS:
                        turn(q + 1)
                    gate(b_z, 1, (wg_hi, wg_lo), u_parts, False, True).then_inc(gz_done, 1)
                    fill(3 * q + 1)

                for q in range(STEPS):
                    if "gru" in on:
                        step(q)
                    else:
                        if "setup" in on and q == SETUP_STEP:
                            setup()
                        for point in range(3 * q, 3 * q + 3):
                            fill(point)

            bodies(pe, body)

        @block.scalar
        def _(act):
            def setup():
                act.wait_ge(weights_in, 16 * 11)
                nc.scalar.activation(wh_hi[:], whht, ACT.Copy).then_inc(setup_act, 1)
                for layer, b in enumerate((b_r, b_z, b_xn, b_hn)):
                    act.wait_ge(setup_pe, layer + 1)
                    nc.scalar.activation(wg_hi[:, layer, :], b[:, 0:G], ACT.Copy).then_inc(setup_act, 1)
                act.wait_ge(setup_pe, L + 2)
                nc.scalar.activation(arow[:, :, :].rearrange("p e c -> p (e c)"), b_u[:, 0:2 * C], ACT.Copy)\
                    .then_inc(setup_copied, 1)
                act.wait_ge(setup_dve, 2)

            def body(pre, gru, post, on):
                def degree(s):
                    act.wait_ge(araw_in[s], 16 * (pre + 1))
                    if s == Y or not (isinstance(pre, int) and pre == 0):
                        act.wait_ge(dd_ready, 2 * pre + s)
                    for t in range(NT):
                        last = nc.scalar.activation(scratch[:, t, :], a_raw[s][:, t, :], ACT.Copy,
                                                    accum_out=deg[:, t:t + 1])
                    last.then_inc(deg_ready, 1)

                def after_gru(s):
                    if s == X and "gru" in on:
                        act.wait_ge(u_done, STEPS * gru + STEPS - 1)
                    if s == Y and not (isinstance(gru, int) and gru == 0):
                        act.wait_ge(u_done, STEPS * gru)

                def split_a(s, h):
                    after_gru(s)
                    for t in half(h):
                        nc.scalar.activation(a_hi[s][:, t, :], a_raw[s][:, t, :], ACT.Copy)\
                            .then_inc(a_hi_ready[s], 1)

                def split_x1(s):
                    after_gru(s)
                    act.wait_ge(x1_ready, 2 * (pre, gru)[s] + s + 1)
                    nc.scalar.activation(hn_hi[s][:], x1[s][:], ACT.Copy).then_inc(x1_hi_ready, 1)

                def agg_copy(kind, s, run, dst):
                    act.wait_ge(agg_done[kind], 2 * run + s + 1)
                    nc.scalar.activation(dst[:], b_agg[:], ACT.Copy).then_inc(agg_copied[kind], 1)

                def agg_l0(s):
                    agg_copy("l0", s, pre, agg_pre)

                def agg_att(s):
                    agg_copy("att", s, post, agg[s])

                def agg_l3(s):
                    agg_copy("l3", s, post, agg[s])

                def att_bcast(s):
                    act.wait_ge(lin_done["bcast"], 2 * post + s + 1)
                    nc.scalar.activation(es[s][:], b_lin[:], ACT.Copy).then_inc(lin_read["bcast"], 1)

                def att_er(s, h):
                    for t in half(h):
                        act.wait_ge(umax_ready, NT * (2 * post + s) + t + 1)
                        nc.scalar.activation(att[s][:, t, :], att[s][:, t, :], ACT.Identity,
                                             bias=ecol[s][:, 1, t:t + 1]).then_inc(logit_ready, 1)

                def att_exp(s, h):
                    g = 2 * post + s
                    act.wait_ge(nmx_ready, g + 1)
                    for t in half(h):
                        act.wait_ge(lrelu_ready, NT * g + t + 1)
                        nc.scalar.activation(att[s][:, t, :], att[s][:, t, :], ACT.Exp, bias=nmx[s][:, t:t + 1],
                                             accum_out=den[s][:, t:t + 1]).then_inc(exp_ready, 1)

                def normalise(kind, s, run, src, dst, ready):
                    k = (flow_of[kind], s)
                    act.wait_ge(shift_ready[kind], 2 * run + s + 1)
                    for t in range(NT):
                        last = nc.scalar.activation(dst[:, t, :], src[:, t, :], ACT.Identity,
                                                    bias=shift[k][:, t:t + 1], scale=rstd[k][:, t:t + 1])
                    last.then_inc(ready, 1)

                def norm_post(s):
                    normalise("post", s, post, x2[s], x2[s], x2_ready)

                def norm_att(s):
                    normalise("att", s, post, x3[s], x3[s], x3_ready)

                def norm_l3(s):
                    normalise("l3", s, post, x2[s], xs[s], out_ready)

                def norm_l0(s):
                    if "gru" in on:
                        act.wait_ge(t_done, STEPS * gru + s + 1)
                        act.wait_ge(res_kept, 2 * gru + s + 1)
                        act.wait_ge(x1_lo_ready, 2 * gru + s + 1)
                    normalise("l0", s, pre, y_pre, x1[s], x1_ready)

                def copy_xT(s):
                    run = (pre, gru)[s]
                    act.wait_ge(t_done, STEPS * run + s + 1)
                    if s == X and "gru" in on:
                        act.wait_ge(back_done, 2 * gru + 1)
                    if s == Y and "post" in on:
                        act.wait_ge(back_done, 2 * post + 2)
                    nc.scalar.activation(hT[s][:], b_t[:], ACT.Copy).then_inc(xT_copied, 1)
                    act.wait_ge(xT_copied, 2 * run + s + 1)
                    split_h(s, run)

                def split_h(q, run):
                    s = q % 2
                    if q >= 2:
                        act.wait_ge(h_ready, STEPS * run + q - 1)
                    nc.scalar.activation(hT_hi[s][:], hT[s][:], ACT.Copy).then_inc(hT_hi_ready, 1)

                pieces = dict(degree=degree, split_x1=split_x1, agg_l0=agg_l0, agg_att=agg_att, agg_l3=agg_l3,
                              att_bcast=att_bcast,
                              norm_post=norm_post, norm_att=norm_att, norm_l3=norm_l3, norm_l0=norm_l0, copy_xT=copy_xT,
                              **in_halves(split_a=split_a, att_er=att_er, att_exp=att_exp))

                def fill(point):
                    for name, s in ACT_FILL.get(point, ()):
                        if flow_of_piece(name, s, ("degree", "agg_l0", "norm_l0")) in on:
                            pieces[name](s)

                def step(q):
                    layer, s = divmod(q, 2)
                    n = STEPS * gru + q
                    act.wait_ge(u_done, n + 1)
                    nc.scalar.activation(uT_hi[s][:], b_u[:], ACT.Copy).then_inc(u_hi_ready, 1)
                    if 2 <= q + 1 < STEPS:
                        split_h(q + 1, gru)
                    fill(3 * q)
                    act.wait_ge(ghn_done, n + 1)
                    nc.scalar.activation(hb[s][:], b_hn[:], ACT.Identity, bias=half_b[:, layer, 2:3], scale=0.5)
                    act.wait_ge(gr_done, n + 1)
                    nc.scalar.activation(rg[s][:], b_r[:], ACT.Tanh, bias=half_b[:, layer, 0:1], scale=0.5)\
                        .then_inc(r_ready, 1)
                    if q == 0:
                        copy_xT(Y)
                    elif q + 1 < STEPS:
                        act.wait_ge(t_done, n + 2)
                        nc.scalar.activation(hn_hi[1 - s][:], tiles(b_t[:]), ACT.Copy).then_inc(hn_hi_ready, 1)
                    act.wait_ge(gz_done, n + 1)
                    nc.scalar.activation(zg[s][:], b_z[:], ACT.Tanh, bias=half_b[:, layer, 1:2], scale=0.5)\
                        .then_inc(ztanh_ready, 1)
                    fill(3 * q + 1)
                    act.wait_ge(pre_n_ready, n + 1)
                    nc.scalar.activation(ng[s][:], hb[s][:], ACT.Tanh, bias=bih[:, layer, 2:3])\
                        .then_inc(n_ready, 1)
                    fill(3 * q + 2)

                for q in range(STEPS):
                    if "gru" in on:
                        step(q)
                    else:
                        if "setup" in on and q == SETUP_STEP:
                            setup()
                        for point in range(3 * q, 3 * q + 3):
                            fill(point)

            bodies(act, body)

        @block.vector
        def _(dve):
            def setup():
                dve.wait_ge(weights_in, 16 * 11)
                dve.wait_ge(setup_pool, 2)
                dve.wait_ge(setup_act, 1)
                nc.vector.tensor_tensor(wh_lo[:], whht, wh_hi[:].bitcast(F32), ALU.subtract)
                for e in range(2):
                    last = nc.vector.tensor_scalar(acols[:, e, :], ones[:], avec[:, e:e + 1], None, ALU.mult)
                last.then_inc(setup_dve, 1)
                nc.vector.tensor_tensor(half_b[:, :, 0:2], bih[:, :, 0:2], bhh[:, :, 0:2], ALU.add)
                nc.vector.tensor_copy(half_b[:, :, 2:3], bhh[:, :, 2:3]).then_inc(setup_copied, 1)
                for layer, b in enumerate((b_r, b_z, b_xn, b_hn)):
                    dve.wait_ge(setup_act, layer + 2)
                    nc.vector.tensor_tensor(wg_lo[:, layer, :], b[:, 0:G], wg_hi[:, layer, :].bitcast(F32),
                                            ALU.subtract).then_inc(setup_copied, 1)
                dve.wait_ge(setup_copied, L + 2)
                nc.vector.tensor_scalar(half_b[:], half_b[:], 0.5, None, ALU.mult).then_inc(setup_dve, 1)

            def body(pre, gru, post, on):
                marks = {"pre": 0, "post": 0}
                runs = {"pre": pre, "post": post}

                def link(flow, ins):
                    marks[flow] += 1
                    ins.then_inc(chain_sem[flow], 1)
                    dve.wait_ge(chain_sem[flow], DVE_LINKS[flow] * runs[flow] + marks[flow])

                def own():
                    dve.wait_ge(setup_dve, 2)

                def statistics(kind, s, src):
                    flow = flow_of[kind]
                    k = (flow, s)
                    for t in range(NT):
                        last = nc.vector.bn_stats(stats[:, t, :], src[:, t, :])
                    link(flow, last)
                    even, odd = stats[:, :, 1:3], stats[:, :, 4:6]
                    nc.vector.tensor_tensor(both[:], even, odd, ALU.add)
                    link(flow, nc.vector.tensor_tensor(dif[:], even[:, :, 0], odd[:, :, 0], ALU.subtract))
                    nc.vector.tensor_scalar(nmean[k][:], both[:, :, 0], -0.5, None, ALU.mult)
                    nc.vector.tensor_scalar(ve[k][:], both[:, :, 1], 1.0 / C, LN_EPS, ALU.mult, ALU.add)
                    link(flow, nc.vector.scalar_tensor_tensor(dif[:], dif[:], 0.25, dif[:],
                                                              ALU.mult, ALU.mult))
                    nc.vector.tensor_tensor(ve[k][:], ve[k][:], dif[:], ALU.add)\
                        .then_inc(var_ready[kind], 1)

                def post_read(s):
                    run = (gru, post)[s]
                    g = 2 * run + s
                    dve.wait_ge(back_done, g + 1)
                    m = nmask[:, bass.ds(g, 1), :].rearrange("p b t -> p (b t)")
                    if not (isinstance(run, int) and run == 0):
                        dve.wait_ge(out_ready, g - 1)
                    nc.vector.tensor_tensor(x2[s][:], tiles(back_bank[s][:]), bc(m), ALU.mult).then_inc(back_read, 1)

                def post_res(s):
                    dve.wait_ge(back_read, 2 * post + s + 1)
                    link("post", nc.vector.tensor_tensor(x2[s][:], x2[s][:], res[s][:], ALU.add))

                def keep_x1(s):
                    dve.wait_ge(x1_ready, 2 * gru + s + 1)
                    nc.vector.tensor_copy(res[s][:], x1[s][:]).then_inc(res_kept, 1)

                def mask(s):
                    dve.wait_ge(at_in[s], 16 * (post + 1))
                    nc.vector.tensor_scalar(att[s][:], at[s][:], 0.0, MASKED, ALU.is_le, ALU.mult)\
                        .then_inc(mask_ready, 1)

                def stats_post(s):
                    statistics("post", s, x2[s])

                def stats_att(s):
                    own()
                    dve.wait_ge(lin_read["att"], 2 * post + s + 1)
                    statistics("att", s, x3[s])

                def stats_l3(s):
                    statistics("l3", s, x2[s])

                def stats_l0(s):
                    dve.wait_ge(x0_used, 2 * pre + s + 1)
                    statistics("l0", s, y_pre)

                def att_scores(s):
                    own()
                    if not (isinstance(post, int) and post == 0):
                        dve.wait_ge(out_stored[s], 16 * post)
                    dve.wait_ge(x2_ready, 2 * post + s + 1)
                    for e in range(2):
                        for t in range(NT):
                            last = nc.vector.tensor_tensor_reduce(
                                out=(tiles(agg[s][:]), xs[s])[e][:, t, :], in0=x2[s][:, t, :],
                                in1=arow[:, e, :], scale=1.0, scalar=0.0,
                                op0=ALU.mult, op1=ALU.add, accum_out=ecol[s][:, e, t:t + 1])
                    link("post", last)
                    nc.vector.tensor_tensor(tiles(es[s][:]), ident[:].unsqueeze(1).to_broadcast([P, NT, P]),
                                            bc(ecol[s][:, 0, :]), ALU.mult).then_inc(ediag_ready, 1)

                def att_max(s, h):
                    g = 2 * post + s
                    own()
                    dve.wait_ge(lin_read["bcast"], g + 1)
                    dve.wait_ge(maskdiag_ready, g + 1)
                    for t in half(h):
                        nc.vector.tensor_tensor_reduce(
                            out=att[s][:, t, :], in0=att[s][:, t, :], in1=es[s][:], scale=1.0, scalar=-3e38,
                            op0=ALU.add, op1=ALU.max, accum_out=mx[s][:, t:t + 1]).then_inc(umax_ready, 1)
                    if h == 1:
                        dve.wait_ge(umax_ready, NT * g + NT)
                        link("post", nc.vector.tensor_tensor(mx[s][:], mx[s][:], ecol[s][:, 1, :], ALU.add))
                        link("post", nc.vector.scalar_tensor_tensor(mx[s][:], mx[s][:], SLOPE, mx[s][:],
                                                                    ALU.mult, ALU.max))
                        nc.vector.tensor_scalar(nmx[s][:], mx[s][:], -1.0, None, ALU.mult).then_inc(nmx_ready, 1)

                def att_lrelu(s, h):
                    g = 2 * post + s
                    for t in half(h):
                        dve.wait_ge(logit_ready, NT * g + t + 1)
                        nc.vector.scalar_tensor_tensor(att[s][:, t, :], att[s][:, t, :], SLOPE, att[s][:, t, :],
                                                       ALU.mult, ALU.max).then_inc(lrelu_ready, 1)

                def att_weight(s):
                    dve.wait_ge(exp_ready, NT * (2 * post + s + 1))
                    link("post", nc.vector.reciprocal(rden[s][:], den[s][:]))
                    nc.vector.tensor_tensor(xs[s][:], x2[s][:], bc(rden[s][:]), ALU.mult).then_inc(xs2_ready, 1)

                def att_res(s):
                    dve.wait_ge(lin_done["att"], 2 * post + s + 1)
                    nc.vector.tensor_tensor(x3[s][:], tiles(b_lin[:]), x2[s][:], ALU.add)\
                        .then_inc(lin_read["att"], 1)

                def att_scale(s):
                    dve.wait_ge(x3_ready, 2 * post + s + 1)
                    nc.vector.tensor_tensor(xs[s][:], x3[s][:], bc(d3_post[:, s, :]), ALU.mult)\
                        .then_inc(xs3_ready, 1)

                def l3_res(s):
                    g = 2 * post + s
                    dve.wait_ge(lin_done["l3"], g + 1)
                    nc.vector.tensor_tensor(x2[s][:], tiles(b_lin[:]), bc(d3_post[:, s, :]), ALU.mult)\
                        .then_inc(lin_read["l3"], 1)
                    dve.wait_ge(lin_read["l3"], g + 1)
                    dve.wait_ge(xb_ready, g + 1)
                    link("post", nc.vector.tensor_tensor(x2[s][:], x2[s][:], x3[s][:], ALU.add))

                def l0_degree(s):
                    g = 2 * pre + s
                    dve.wait_ge(adiag_ready, g + 1)
                    link("pre", nc.vector.reduce_sum(ann[:], adiag[:], AX_X))
                    dve.wait_ge(deg_ready, g + 1)
                    link("pre", nc.vector.tensor_tensor(ann[:], deg[:], ann[:], ALU.subtract))
                    nc.vector.tensor_scalar(dd[:, 0:NT], ann[:], 1.0, None, ALU.add)
                    nc.vector.tensor_scalar(dd[:, NT:2 * NT], deg[:], DEG_EPS, None, ALU.add)\
                        .then_inc(dd_ready, 1)

                def l0_scale(s):
                    g = 2 * pre + s
                    dve.wait_ge(ddp_ready, g + 1)
                    link("pre", nc.vector.tensor_scalar(d0[:], ddp[:, 0:NT], DEG_EPS, None, ALU.add))
                    link("pre", nc.vector.reciprocal(d0[:], d0[:]))
                    nc.vector.tensor_copy(d3_pre[:, s, :], ddp[:, NT:2 * NT])
                    dve.wait_ge(x0_in[s], 16 * (pre + 1))
                    if s == Y or not (isinstance(pre, int) and pre == 0):
                        dve.wait_ge(agg_done["l0"], g)
                        dve.wait_ge(x1_ready, g)
                    nc.vector.tensor_tensor(xs_pre[:], x0[s][:], bc(d0[:]), ALU.mult).then_inc(xs0_ready, 1)

                def l0_res(s):
                    g = 2 * pre + s
                    dve.wait_ge(lin_done["l0"], g + 1)
                    nc.vector.tensor_tensor(y_pre[:], tiles(b_lin[:]), bc(d0[:]), ALU.mult)\
                        .then_inc(lin_read["l0"], 1)
                    dve.wait_ge(lin_read["l0"], g + 1)
                    nc.vector.scalar_tensor_tensor(y_pre[:], y_pre[:], 0.0, x0[s][:], ALU.max, ALU.add)\
                        .then_inc(x0_used, 1)

                def split_x1(s):
                    dve.wait_ge(x1_hi_ready, 2 * (pre, gru)[s] + s + 1)
                    nc.vector.tensor_tensor(hn_lo[s][:], x1[s][:], hn_hi[s][:].bitcast(F32), ALU.subtract)\
                        .then_inc(x1_lo_ready, 1)

                pieces = dict(post_read=post_read, post_res=post_res, keep_x1=keep_x1, mask=mask,
                              att_scores=att_scores, att_weight=att_weight, att_res=att_res, att_scale=att_scale,
                              l3_res=l3_res, l0_degree=l0_degree, l0_scale=l0_scale, l0_res=l0_res,
                              split_x1=split_x1, stats_post=stats_post, stats_att=stats_att, stats_l3=stats_l3,
                              stats_l0=stats_l0, **in_halves(att_max=att_max, att_lrelu=att_lrelu))
                of_pre = ("l0_degree", "l0_scale", "l0_res", "stats_l0")

                def fill(point):
                    for name, s in DVE_FILL.get(point, ()):
                        if flow_of_piece(name, s, of_pre) in on:
                            pieces[name](s)

                def step(q):
                    s = q % 2
                    n = STEPS * gru + q
                    dve.wait_ge(u_hi_ready, n + 1)
                    nc.vector.tensor_tensor(uT_lo[s][:], b_u[:], uT_hi[s][:].bitcast(F32), ALU.subtract)\
                        .then_inc(u_lo_ready, 1)
                    fill(3 * q)
                    dve.wait_ge(r_ready, n + 1)
                    nc.vector.scalar_tensor_tensor(hb[s][:], rg[s][:], 1.0, hb[s][:], ALU.add, ALU.mult)\
                        .then_inc(t_ready, 1)
                    dve.wait_ge(gxn_done, n + 1)
                    dve.wait_ge(t_ready, n + 1)
                    nc.vector.tensor_tensor(hb[s][:], b_xn[:], hb[s][:], ALU.add).then_inc(pre_n_ready, 1)
                    if 2 <= q + 1 < STEPS:
                        dve.wait_ge(hn_hi_ready, (STEPS - 2) * gru + q)
                        nc.vector.tensor_tensor(hn_lo[1 - s][:], tiles(b_t[:]), hn_hi[1 - s][:].bitcast(F32),
                                                ALU.subtract).then_inc(hn_lo_ready, 1)
                    fill(3 * q + 1)
                    dve.wait_ge(n_ready, n + 1)
                    dve.wait_ge(z_ready, n + 1)
                    nc.vector.scalar_tensor_tensor(ng[s][:], zg[s][:], 1.0, ng[s][:], ALU.subtract, ALU.mult)\
                        .then_inc(w_ready, 1)
                    dve.wait_ge(w_ready, n + 1)
                    dve.wait_ge(zh_ready, n + 1)
                    nc.vector.tensor_tensor(hT[s][:], zh[s][:], ng[s][:], ALU.subtract).then_inc(h_ready, 1)
                    fill(3 * q + 2)

                if "post" in on:
                    link("post", nc.vector.tensor_copy(d3_post[:], d3_gru[:]))
                if "gru" in on:
                    nc.vector.tensor_copy(d3_gru[:], d3_pre[:])
                fill(-1)
                for q in range(STEPS):
                    if "gru" in on:
                        step(q)
                    else:
                        if "setup" in on and q == SETUP_STEP:
                            setup()
                        for point in range(3 * q, 3 * q + 3):
                            fill(point)
                for flow in ("pre", "post"):
                    assert flow not in on or marks[flow] == DVE_LINKS[flow], (flow, marks[flow])

            bodies(dve, body)

        @block.gpsimd
        def _(pool):
            nc.gpsimd.memset(ones[:], 1.0).then_inc(setup_pool, 1)
            pool.wait_ge(setup_pool, 1)
            nc.gpsimd.affine_select(out=ident[:], in_=ones[:], compare_op=ALU.is_equal, fill=0.0, base=0,
                                    pattern=[[-1, P]], channel_multiplier=1).then_inc(setup_pool, 1)
            nc.gpsimd.memset(exps[:, 0:NT], 0.5).then_inc(setup_pool, 1)
            nc.gpsimd.memset(exps[:, NT:2 * NT], -0.5).then_inc(setup_pool, 1)
            pool.wait_ge(setup_pool, 4)

            def setup():
                pool.wait_ge(weights_in, 16 * 11)

            def body(pre, gru, post, on):
                runs = {"pre": pre, "post": post}

                def one_diagonal(m, value, ready):
                    d = diagonal(m)
                    nc.gpsimd.affine_select(out=d, in_=d, compare_op=ALU.not_equal, fill=value, base=0,
                                            pattern=[[0, NT], [-1, P]], channel_multiplier=1).then_inc(ready, 1)

                def wait_apart(sem, count):
                    count = count if isinstance(count, int) else pool.to_reg(count)
                    pool.wait_ge(setup_pool, 4)
                    pool.wait_ge(sem, count)

                def diag_a(s):
                    pool.wait_ge(araw_in[s], 16 * (pre + 1))
                    if s == Y or not (isinstance(pre, int) and pre == 0):
                        pool.wait_ge(dd_ready, 2 * pre + s)
                    nc.gpsimd.tensor_tensor(adiag[:], diagonal(a_raw[s]), ident[:].unsqueeze(1)
                                            .to_broadcast([P, NT, P]), ALU.mult).then_inc(adiag_ready, 1)

                def diag_at(s):
                    wait_apart(atpre_in, 16 * (2 * pre + s + 1))
                    one_diagonal(at_pre, 1.0, atdiag_ready)

                def split_a(s, h):
                    for t in half(h):
                        pool.wait_ge(a_hi_ready[s], NT * (pre, gru)[s] + t + 1)
                        nc.gpsimd.tensor_tensor(a_lo[s][:, t, :], a_raw[s][:, t, :], a_hi[s][:, t, :].bitcast(F32),
                                                ALU.subtract).then_inc(a_lo_ready[s], 1)

                def powers(s):
                    pool.wait_ge(dd_ready, 2 * pre + s + 1)
                    nc.gpsimd.tensor_tensor(ddp[:], dd[:], exps[:], ALU.pow).then_inc(ddp_ready, 1)

                def mask_diag(s):
                    wait_apart(mask_ready, 2 * post + s + 1)
                    one_diagonal(att[s], 0.0, maskdiag_ready)

                def add_bias(s):
                    pool.wait_ge(xs3_ready, 2 * post + s + 1)
                    nc.gpsimd.tensor_tensor(x3[s][:], x3[s][:], bias3[:].unsqueeze(1)
                                            .to_broadcast([P, NT, C]), ALU.add).then_inc(xb_ready, 1)

                def rstd_of(kind):
                    flow = flow_of[kind]

                    def piece(s):
                        k, n = (flow, s), 2 * runs[flow] + s + 1
                        pool.wait_ge(var_ready[kind], n)
                        nc.gpsimd.tensor_tensor(rstd[k][:], ve[k][:], exps[:, NT:2 * NT], ALU.pow)\
                            .then_inc(rstd_ready[kind], 1)
                        pool.wait_ge(rstd_ready[kind], n)
                        nc.gpsimd.tensor_tensor(shift[k][:], nmean[k][:], rstd[k][:], ALU.mult)\
                            .then_inc(shift_ready[kind], 1)
                    return piece

                def split_h(q, run):
                    pool.wait_ge(hT_hi_ready, STEPS * run + q + 1)
                    nc.gpsimd.tensor_tensor(hT_lo[q % 2][:], hT[q % 2][:], hT_hi[q % 2][:].bitcast(F32),
                                            ALU.subtract).then_inc(hT_lo_ready, 1)

                def split_xT(s):
                    split_h(0, pre)

                pieces = dict(diag_a=diag_a, diag_at=diag_at, powers=powers, mask_diag=mask_diag,
                              add_bias=add_bias, split_xT=split_xT,
                              **{f"rstd_{k}": rstd_of(k) for k in ("post", "att", "l3", "l0")},
                              **in_halves(split_a=split_a))
                of_pre = ("diag_a", "diag_at", "powers", "rstd_l0")

                def fill(point):
                    for name, s in POOL_FILL.get(point, ()):
                        if flow_of_piece(name, s, of_pre) in on:
                            pieces[name](s)

                for q in range(STEPS):
                    if "gru" in on:
                        n, s = STEPS * gru + q, q % 2
                        if 2 <= q + 1 < STEPS:
                            split_h(q + 1, gru)
                        fill(3 * q)
                        if q == 0:
                            split_h(1, gru)
                        wait_apart(ztanh_ready, n + 1)
                        nc.gpsimd.tensor_scalar(zg[s][:], zg[s][:], 0.5, 0.5, ALU.mult, ALU.add)\
                            .then_inc(z_ready, 1)
                        pool.wait_ge(z_ready, n + 1)
                        nc.gpsimd.tensor_tensor(zh[s][:], zg[s][:], hT[s][:], ALU.mult).then_inc(zh_ready, 1)
                    else:
                        if "setup" in on and q == SETUP_STEP:
                            setup()
                        fill(3 * q)
                    fill(3 * q + 1)
                    fill(3 * q + 2)

            bodies(pool, body)


def kernel(x, adj, nodemask, L0_gnn_kernel, L1_gnn_weight, L1_gnn_w_ih, L1_gnn_w_hh, L1_gnn_b_ih, L1_gnn_b_hh,
           L2_gnn_W_pre, L2_gnn_a_snd, L2_gnn_a_rec, L3_gnn_weight, L3_gnn_bias):
    import numpy as np
    import concourse.bacc as bacc
    from concourse import mybir as mb
    from concourse.bass_utils import run_bass_kernel_spmd as run

    x, adj = np.asarray(x), np.asarray(adj)
    B, N, C = x.shape
    P = 128
    NT = N // P

    def tiled(m):
        return m.reshape(B, NT, P, m.shape[-1]).transpose(0, 2, 1, 3)

    L = np.asarray(L1_gnn_weight).shape[0]
    arrays = {
        "x": tiled(x),
        "adj": tiled(adj),
        "adjt": tiled(adj.transpose(0, 2, 1)),
        "nodemask": np.asarray(nodemask).reshape(B, NT, P).transpose(2, 0, 1),
        "k0": np.asarray(L0_gnn_kernel),
        "w1t": np.asarray(L1_gnn_weight).transpose(2, 0, 1),
        "wiht": np.asarray(L1_gnn_w_ih).transpose(2, 0, 1),
        "whht": np.asarray(L1_gnn_w_hh).transpose(2, 0, 1),
        "bih": np.asarray(L1_gnn_b_ih).reshape(L, 3, C).transpose(2, 0, 1),
        "bhh": np.asarray(L1_gnn_b_hh).reshape(L, 3, C).transpose(2, 0, 1),
        "wpre": np.asarray(L2_gnn_W_pre),
        "wpret": np.asarray(L2_gnn_W_pre).T,
        "avec": np.stack([np.asarray(L2_gnn_a_snd), np.asarray(L2_gnn_a_rec)], axis=1),
        "w3": np.asarray(L3_gnn_weight),
        "bias3": np.asarray(L3_gnn_bias).reshape(1, C),
    }
    arrays = {f"in_{k}": np.ascontiguousarray(v) for k, v in arrays.items()}
    nc = bacc.Bacc("TRN2", target_bir_lowering=False, num_devices=1)
    ins = [nc.dram_tensor(k, v.shape, mb.dt.from_np(v.dtype), kind="ExternalInput").ap() for k, v in arrays.items()]
    out = nc.dram_tensor("out", (B, P, NT, C), mb.dt.float32, kind="ExternalOutput").ap()
    gnn_kernel(nc, *ins, out)
    got = run(nc, [arrays], core_ids=[0]).results[0]["out"]
    return np.ascontiguousarray(got.transpose(0, 2, 1, 3).reshape(B, N, C))
```
